# Optimizing a Trainium2 kernel written in Bass

```python
import numpy as np
import jax
import jax.numpy as jnp

def _softmax(x, axis=-1):
    return jax.nn.softmax(x, axis=axis)

def _gelu(x):
    return jax.nn.gelu(x, approximate=True)

def _silu(x):
    return jax.nn.silu(x)

def _sigmoid(x):
    return jax.nn.sigmoid(x)

def _layernorm(x, axis=-1, eps=1e-05):
    m = jnp.mean(x, axis=axis, keepdims=True)
    v = jnp.var(x, axis=axis, keepdims=True)
    return (x - m) / jnp.sqrt(v + eps)

def _scatter_add(tgt, idx, src, axis=0):
    return tgt.at[idx].add(src)

def _segment_sum(src, seg, n):
    return jax.ops.segment_sum(src, seg, n)
kernel_name = 'mk_macaron_d1_jaxref_r8_c641a3'

def setup_inputs(seed: int=0):
    np.random.seed(seed)
    _w = jnp.asarray

    def _L0_attn_setup():
        import math
        import jax, jax.numpy as jnp
        import numpy as np
        HEADS = 16
        DIM_HEAD = 64
        NUM_NULL_KV = 2
        ATTN_SCALE = 8.0
        LN_EPS = 1e-05

        def _alibi_slopes(heads):
            start = 2.0 ** (-2.0 ** (-(math.log2(heads) - 3.0)))
            return np.array([start * start ** i for i in range(heads)], dtype=np.float32)

        def _l2norm(t):
            return t / jnp.maximum(jnp.linalg.norm(t, axis=-1, keepdims=True), 1e-12)
        key = jax.random.key(seed)
        ks = jax.random.split(key, 5)
        b, n, dim = (4, 256, 128)
        return {'x': jax.random.normal(ks[0], (b, n, dim), dtype=jnp.float32), 'gamma': jnp.ones((dim,), dtype=jnp.float32), 'w_q': jax.random.normal(ks[1], (dim, HEADS * DIM_HEAD), dtype=jnp.float32) * 0.02, 'w_kv': jax.random.normal(ks[2], (dim, 2 * HEADS * DIM_HEAD), dtype=jnp.float32) * 0.02, 'null_kv': jax.random.normal(ks[3], (HEADS, 2 * NUM_NULL_KV, DIM_HEAD), dtype=jnp.float32), 'q_scale': jnp.ones((DIM_HEAD,), dtype=jnp.float32), 'k_scale': jnp.ones((DIM_HEAD,), dtype=jnp.float32), 'w_out': jax.random.normal(ks[4], (HEADS * DIM_HEAD, dim), dtype=jnp.float32) * 0.02}
    _L0_attn_in = _L0_attn_setup()

    def _L0_ffn_setup():
        import jax, jax.numpy as jnp
        import numpy as np
        DM, NEXPERTS, SETS, ESIZE = (128, 32, 4, 32)
        B, S = (2, 1024)
        key = jax.random.key(seed)
        ks = jax.random.split(key, 7)
        sc = 0.02
        return {'x': jax.random.normal(ks[0], (B, S, DM), jnp.float32), 'Wc': jax.random.normal(ks[1], (DM, NEXPERTS, SETS), jnp.float32) * sc, 'bc': jax.random.normal(ks[2], (NEXPERTS, SETS), jnp.float32) * sc, 'W1': jax.random.normal(ks[3], (NEXPERTS, SETS, DM, ESIZE), jnp.float32) * sc, 'b1': jax.random.normal(ks[4], (NEXPERTS, SETS, ESIZE), jnp.float32) * sc, 'W2': jax.random.normal(ks[5], (NEXPERTS, SETS, DM, ESIZE), jnp.float32) * sc, 'b2': jax.random.normal(ks[6], (NEXPERTS, SETS, DM), jnp.float32) * sc}
    _L0_ffn_in = _L0_ffn_setup()
    _d = {'L0_attn_x': _L0_attn_in['x'], 'L0_attn_gamma': _L0_attn_in['gamma'], 'L0_attn_w_q': _L0_attn_in['w_q'], 'L0_attn_w_kv': _L0_attn_in['w_kv'], 'L0_attn_null_kv': _L0_attn_in['null_kv'], 'L0_attn_q_scale': _L0_attn_in['q_scale'], 'L0_attn_k_scale': _L0_attn_in['k_scale'], 'L0_attn_w_out': _L0_attn_in['w_out'], 'L0_ffn_Wc': _L0_ffn_in['Wc'], 'L0_ffn_bc': _L0_ffn_in['bc'], 'L0_ffn_W1': _L0_ffn_in['W1'], 'L0_ffn_b1': _L0_ffn_in['b1'], 'L0_ffn_W2': _L0_ffn_in['W2'], 'L0_ffn_b2': _L0_ffn_in['b2']}
    _x0 = _d['L0_attn_x']
    _d['L0_attn_x'] = jax.random.normal(jax.random.fold_in(jax.random.key(seed), 1), (4, 1024, 128), dtype=_x0.dtype)
    del _x0
    return _d

def reference(L0_attn_x, L0_attn_gamma, L0_attn_w_q, L0_attn_w_kv, L0_attn_null_kv, L0_attn_q_scale, L0_attn_k_scale, L0_attn_w_out, L0_ffn_Wc, L0_ffn_bc, L0_ffn_W1, L0_ffn_b1, L0_ffn_W2, L0_ffn_b2):

    def _L0_attn_ref(x, gamma, w_q, w_kv, null_kv, q_scale, k_scale, w_out):
        import math
        import jax, jax.numpy as jnp
        import numpy as np
        HEADS = 16
        DIM_HEAD = 64
        NUM_NULL_KV = 2
        ATTN_SCALE = 8.0
        LN_EPS = 1e-05

        def _alibi_slopes(heads):
            start = 2.0 ** (-2.0 ** (-(math.log2(heads) - 3.0)))
            return np.array([start * start ** i for i in range(heads)], dtype=np.float32)

        def _l2norm(t):
            return t / jnp.maximum(jnp.linalg.norm(t, axis=-1, keepdims=True), 1e-12)
        b, n, dim = x.shape
        mu = jnp.mean(x, axis=-1, keepdims=True)
        var = jnp.mean(jnp.square(x - mu), axis=-1, keepdims=True)
        xn = (x - mu) * jax.lax.rsqrt(var + LN_EPS) * gamma
        q = (xn @ w_q).reshape(b, n, HEADS, DIM_HEAD).transpose(0, 2, 1, 3)
        kv = xn @ w_kv
        k, v = jnp.split(kv, 2, axis=-1)
        k = k.reshape(b, n, HEADS, DIM_HEAD).transpose(0, 2, 1, 3)
        v = v.reshape(b, n, HEADS, DIM_HEAD).transpose(0, 2, 1, 3)
        nkv = null_kv.reshape(HEADS, NUM_NULL_KV, 2, DIM_HEAD)
        nk = jnp.broadcast_to(nkv[:, :, 0][None], (b, HEADS, NUM_NULL_KV, DIM_HEAD))
        nv = jnp.broadcast_to(nkv[:, :, 1][None], (b, HEADS, NUM_NULL_KV, DIM_HEAD))
        k = jnp.concatenate([nk, k], axis=2)
        v = jnp.concatenate([nv, v], axis=2)
        q = _l2norm(q) * q_scale
        k = _l2norm(k) * k_scale
        sim = jnp.einsum('bhid,bhjd->bhij', q, k) * ATTN_SCALE
        j = n + NUM_NULL_KV
        rows = jnp.arange(n)
        cols = jnp.arange(j)
        dist = -jnp.abs(cols[None, :] - (rows[:, None] + NUM_NULL_KV)).astype(sim.dtype)
        slopes = jnp.asarray(_alibi_slopes(HEADS))
        sim = sim + dist[None, None] * slopes[None, :, None, None]
        causal_mask = cols[None, :] > rows[:, None] + NUM_NULL_KV
        neg = -jnp.finfo(sim.dtype).max
        sim = jnp.where(causal_mask[None, None], neg, sim)
        attn = jax.nn.softmax(sim, axis=-1)
        out = jnp.einsum('bhij,bhjd->bhid', attn, v)
        out = out.transpose(0, 2, 1, 3).reshape(b, n, HEADS * DIM_HEAD)
        return out @ w_out

    def _L0_ffn_ref(x, Wc, bc, W1, b1, W2, b2):
        import jax, jax.numpy as jnp
        import numpy as np
        DM, NEXPERTS, SETS, ESIZE = (128, 32, 4, 32)
        B, S = (2, 1024)
        b, s, d = x.shape
        g = Wc.shape[1]
        grouped = x.reshape(b, s // g, g, d)
        logits = jnp.einsum('bntd,des->bntes', grouped, Wc) + bc
        tie = jnp.linspace(0.0, 1e-06, g, dtype=x.dtype).reshape(-1, 1, 1)
        logits = logits + tie
        perm = (logits == jnp.max(logits, axis=-3, keepdims=True)).astype(x.dtype)
        permuted = jnp.einsum('bntd,bntes->bnesd', grouped, perm)
        inner = jax.nn.relu(jnp.einsum('bnesd,esdf->bnesf', permuted, W1) + b1)
        result_permuted = jnp.einsum('bnesf,esdf->bnesd', inner, W2) + b2
        result = jnp.einsum('bnesd,bntes->bntd', result_permuted, perm)
        return result.reshape(b, s, d)
    x = L0_attn_x
    x = x + 0.5 * _L0_ffn_ref(_layernorm(x, axis=-1), L0_ffn_Wc, L0_ffn_bc, L0_ffn_W1, L0_ffn_b1, L0_ffn_W2, L0_ffn_b2)
    x = x + _L0_attn_ref(_layernorm(x, axis=-1), L0_attn_gamma, L0_attn_w_q, L0_attn_w_kv, L0_attn_null_kv, L0_attn_q_scale, L0_attn_k_scale, L0_attn_w_out)
    x = x + 0.5 * _L0_ffn_ref(_layernorm(x, axis=-1), L0_ffn_Wc, L0_ffn_bc, L0_ffn_W1, L0_ffn_b1, L0_ffn_W2, L0_ffn_b2)
    return x

_drawn_inputs = setup_inputs


def setup_inputs(seed=0):
    import zlib

    import numpy as np

    out = dict(_drawn_inputs(seed))
    spreads = {'L0_attn_gamma': (1.0, 0.6), 'L0_attn_q_scale': (1.0, 0.6), 'L0_attn_k_scale': (1.0, 0.6)}
    factors = {'L0_ffn_b1': 8.0}
    for name, (base, spread) in spreads.items():
        noise = np.random.default_rng([zlib.crc32(name.encode()), seed]).standard_normal(out[name].shape)
        drawn = base * np.exp(spread * noise) if base else spread * noise
        out[name] = jnp.asarray(drawn.astype(out[name].dtype))
    for name, factor in factors.items():
        out[name] = (out[name] * factor).astype(out[name].dtype)
    return out
```

```python
from contextlib import ExitStack

import concourse.bass as bass
from concourse import mybir

F32 = mybir.dt.float32
F32R = mybir.dt.float32r
I32 = mybir.dt.int32
ALU = mybir.AluOpType
ACT = mybir.ActivationFunctionType
AX = mybir.AxisListType
P = 128
EPS = 1e-5


def newton_rsqrt(ops, eng, step, out, v, tmp):
    bits = out.bitcast(I32)
    ops.tensor_scalar(bits, v.bitcast(I32), -0.5, float(0x5F3759DF), ALU.mult, ALU.add).then_inc(step, 1)
    eng.wait_ge(step, 1).then_inc(step, -1)
    for _ in range(3):
        ops.tensor_tensor(tmp, out, out, ALU.mult).then_inc(step, 1)
        eng.wait_ge(step, 1).then_inc(step, -1)
        ops.tensor_tensor(tmp, tmp, v, ALU.mult).then_inc(step, 1)
        eng.wait_ge(step, 1).then_inc(step, -1)
        ops.tensor_scalar(tmp, tmp, -0.5, 1.5, ALU.mult, ALU.add).then_inc(step, 1)
        eng.wait_ge(step, 1).then_inc(step, -1)
        ops.tensor_tensor(out, tmp, out, ALU.mult).then_inc(step, 1)
        eng.wait_ge(step, 1).then_inc(step, -1)


def tile_stats(nc, dve, step, src, first, bn, mv, stats):
    for k in range(4):
        ins = nc.vector.bn_stats(bn[:, k, :], src[:, bass.ds(first + k, 1), :])
    ins.then_inc(step, 1)
    dve.wait_ge(step, 1).then_inc(step, -1)
    for k in range(4):
        ins = nc.vector.bn_aggr(mv[:, k, :], bn[:, k, :])
    ins.then_inc(step, 1)
    dve.wait_ge(step, 1).then_inc(step, -1)
    nc.vector.tensor_copy(stats[:, bass.ds(first, 4), :], mv[:, :, :]).then_inc(step, 1)
    dve.wait_ge(step, 1).then_inc(step, -1)


def ffn(nc, x, ident, dram, pre):
    Wc, bc, W1, b1, W2, b2 = dram
    NE, NS, D, F = W1.shape
    ES = NE * NS
    TILES = x.shape[1]
    GROUP = 32
    PER = P // GROUP
    NG = TILES * PER
    with ExitStack() as ctx:
        sb = lambda n, s, d=F32: ctx.enter_context(nc.sbuf_tensor(pre + n, s, d))
        pb = lambda n, s: ctx.enter_context(nc.psum_tensor(pre + n, s, F32))
        sem = lambda n: ctx.enter_context(nc.semaphore(pre + n))

        G = sb("G", [P, ES, NG])
        R = sb("R", [P, NG, ES])
        permT = sb("permT", [P, TILES, P])
        stats = sb("stats", [P, TILES, 2])
        bn = sb("bn", [P, 4, 6])
        mv = sb("mv", [P, 4, 2])
        var = sb("var", [P, TILES])
        rstd = sb("rstd", [P, TILES])
        tmp = sb("tmp", [P, TILES])
        wc = sb("wc", [P, ES])
        bcol = sb("bcol", [P, 1])
        tie = sb("tie", [P, 4 * P])
        tie_i = sb("tie_i", [P, 4 * P], I32)
        blk = sb("blk", [P, PER, P])
        z = sb("z", [P, 4, P])
        zT = sb("zT", [P, 4 * P])
        L = sb("L", [P, 4 * P])
        top = sb("top", [P, 16])
        bd = sb("bd", [P, 2, PER, P])
        w1 = sb("w1", [P, 2, NS, F])
        w2 = sb("w2", [P, 2, NS, F])
        w2T = sb("w2T", [P, P])
        b1r = sb("b1r", [NE, NS * F])
        b2r = sb("b2r", [ES, P])
        b1T = sb("b1T", [P, NE])
        b2T = sb("b2T", [P, ES])
        b1e = sb("b1e", [P, 2])
        b2e = sb("b2e", [P, 2, NS])
        h = sb("h", [P, NS * NG])
        hb = sb("hb", [P, NS, P])
        Rs = sb("Rs", [P, 2, PER, P])
        pT = sb("pT", [P, 2, P])
        Rt = sb("Rt", [P, PER, P])
        pT4 = sb("pT4", [P, 4, P])

        ps = [pb(f"ps{i}", [P, 4 * P]) for i in range(8)]

        loaded = sem("loaded")
        iota_done = sem("iota_done")
        consts = sem("consts")
        step = sem("step")
        z_ready = sem("z_ready")
        zT_full = sem("zT_full")
        zT_ready = sem("zT_ready")
        logits = sem("logits")
        perm_ready = sem("perm_ready")
        perm_full = sem("perm_full")
        bd_ready = sem("bd_ready")
        g_full = [sem(f"g_full{i}") for i in range(2)]
        g_free = [sem(f"g_free{i}") for i in range(2)]
        setup_full = sem("setup_full")
        setup_done = sem("setup_done")
        g_done = sem("g_done")
        w_loaded = [sem(f"w_loaded{i}") for i in range(2)]
        w_free = [sem(f"w_free{i}") for i in range(2)]
        w2_full = sem("w2_full")
        w2T_ready = sem("w2T_ready")
        bias_ready = sem("bias_ready")
        bias_ready2 = sem("bias_ready2")
        h_full = sem("h_full")
        h_ready = sem("h_ready")
        hb_ready = sem("hb_ready")
        r_full = sem("r_full")
        bias_free = sem("bias_free")
        bias_free2 = sem("bias_free2")
        r_done = sem("r_done")
        st_loaded = [sem(f"st_loaded{i}") for i in range(2)]
        st_free = [sem(f"st_free{i}") for i in range(2)]
        rt_full = sem("rt_full")
        rt_ready = sem("rt_ready")
        y_full = sem("y_full")
        y_free = sem("y_free")
        r_summed = sem("r_summed")
        bd_used = sem("bd_used")

        block = ctx.enter_context(nc.Block(pre + "blk"))

        @block.sync
        def _(sp):
            sp.dma_start(wc[:, :], Wc.rearrange("d e s -> d (e s)")).then_inc(loaded, 16)
            sp.dma_start(bcol[:, :], bc.rearrange("e s -> (e s)").unsqueeze(1)).then_inc(loaded, 16)
            sp.dma_start(b1r[:, :], b1.rearrange("e s f -> e (s f)")).then_inc(loaded, 16)
            sp.dma_start(b2r[:, :], b2.rearrange("e s d -> (e s) d")).then_inc(loaded, 16)
            with sp.Fori(0, NE // 2) as i:
                for k in range(2):
                    sp.wait_ge(w_free[k], 1).then_inc(w_free[k], -1)
                    for dst, src in ((w1, W1), (w2, W2)):
                        sp.dma_start(dst[:, k, :, :], src[bass.ds(2 * i + k, 1)].rearrange("a s d f -> d (a s) f")).then_inc(w_loaded[k], 16)
            sp.wait_ge(r_done, 1).then_inc(r_done, -1)
            with sp.Fori(0, TILES // 2) as i:
                for k in range(2):
                    sp.wait_ge(st_free[k], 1).then_inc(st_free[k], -1)
                    sp.dma_start(Rs[:, k, :, :], R[:, bass.ds((2 * i + k) * PER, PER), :]).then_inc(st_loaded[k], 16)
                    sp.dma_start(pT[:, k, :], permT[:, bass.ds(2 * i + k, 1), :]).then_inc(st_loaded[k], 16)

        @block.gpsimd
        def _(pool):
            nc.gpsimd.iota(tie_i[:, :], [[0, 16], [1, GROUP]], base=0, channel_multiplier=0).then_inc(iota_done, 1)
            nc.gpsimd.memset(blk[:, :, :], 1.0).then_inc(iota_done, 1)
            pool.wait_ge(iota_done, 2)
            nc.gpsimd.affine_select(out=blk[:, :, :], in_=blk[:, :, :], compare_op=ALU.is_ge, fill=0.0, base=0, pattern=[[-GROUP, PER], [0, P]], channel_multiplier=1).then_inc(iota_done, 1)
            pool.wait_ge(iota_done, 3)
            nc.gpsimd.affine_select(out=blk[:, :, :], in_=blk[:, :, :], compare_op=ALU.is_ge, fill=0.0, base=GROUP - 1, pattern=[[GROUP, PER], [0, P]], channel_multiplier=-1).then_inc(consts, 1)
            pool.wait_ge(setup_done, 1).then_inc(setup_done, -1)
            with pool.Fori(0, NE // 2) as i:
                for k in range(2):
                    pool.wait_ge(bias_free, 1).then_inc(bias_free, -1)
                    pool.wait_ge(bias_free2, 1).then_inc(bias_free2, -1)
                    nc.gpsimd.tensor_copy(b1e[:, k:k + 1], b1T[:, bass.ds(2 * i + k, 1)]).then_inc(bias_ready, 1)
                    nc.gpsimd.tensor_copy(b2e[:, k, :], b2T[:, bass.ds((2 * i + k) * NS, NS)]).then_inc(bias_ready2, 1)

        @block.tensor
        def _(pe):
            pe.wait_ge(loaded, 64)
            nc.tensor.transpose(ps[7][:, 0:NE], b1r[:, :], ident[0:NE, 0:NE])
            nc.tensor.transpose(ps[7][:, P:P + ES], b2r[:, :], ident[:, :]).then_inc(setup_full, 1)
            with pe.Fori(0, TILES // 4) as i:
                pe.wait_ge(z_ready, 1).then_inc(z_ready, -1)
                for t in range(4):
                    ins = nc.tensor.transpose(ps[0][:, P * t:P * t + P], z[:, t, :], ident[:, :])
                ins.then_inc(zT_full, 1)
                pe.wait_ge(zT_ready, 1).then_inc(zT_ready, -1)
                nc.tensor.matmul(ps[1][:, :], wc[:, :], zT[:, :], start=True, stop=True).then_inc(logits, 1)
                pe.wait_ge(perm_ready, 1).then_inc(perm_ready, -1)
                for t in range(4):
                    ins = nc.tensor.transpose(ps[2][:, P * t:P * t + P], pT4[:, t, :], ident[:, :])
                ins.then_inc(perm_full, 1)
                for t in range(4):
                    pe.wait_ge(bd_ready, 1).then_inc(bd_ready, -1)
                    pe.wait_ge(g_free[t % 2], 1).then_inc(g_free[t % 2], -1)
                    nc.tensor.matmul(ps[3 + t % 2][:, :], z[:, t, :], bd[:, t % 2, :, :], start=True, stop=True).then_inc(g_full[t % 2], 1)
            pe.wait_ge(g_done, 1).then_inc(g_done, -1)
            with pe.Fori(0, NE // 2) as i:
                for k in range(2):
                    pe.wait_ge(w_loaded[k], 32).then_inc(w_loaded[k], -32)
                    nc.tensor.transpose(ps[0][:, 0:P], w2[:, k, :, :], ident[:, :]).then_inc(w2_full, 1)
                    nc.tensor.matmul(ps[1][:, :], w1[:, k, :, :], G[:, bass.ds((2 * i + k) * NS, NS), :], start=True, stop=True).then_inc(h_full, 1)
                    pe.wait_ge(w2T_ready, 1).then_inc(w2T_ready, -1)
                    pe.wait_ge(hb_ready, 1).then_inc(hb_ready, -1)
                    nc.tensor.matmul(ps[2][:, :], w2T[:, :], hb[:, :, :], start=True, stop=True).then_inc(r_full, 1)
            with pe.Fori(0, TILES // 2) as i:
                for k in range(2):
                    pe.wait_ge(st_loaded[k], 32).then_inc(st_loaded[k], -32)
                    for g in range(PER):
                        ins = nc.tensor.transpose(ps[3][:, P * g:P * g + P], Rs[:, k, g, :], ident[:, :])
                    ins.then_inc(rt_full, 1)
                    pe.wait_ge(rt_ready, 1).then_inc(rt_ready, -1)
                    pe.wait_ge(y_free, 1).then_inc(y_free, -1)
                    for g in range(PER):
                        ins = nc.tensor.matmul(ps[4][GROUP * g:GROUP * g + GROUP, 0:P], pT[:, k, GROUP * g:GROUP * g + GROUP], Rt[:, g, :], start=True, stop=True)
                    ins.then_inc(y_full, 1)

        @block.scalar
        def _(act):
            act.wait_ge(setup_full, 1).then_inc(setup_full, -1)
            nc.scalar.copy(b1T[:, :], ps[7][:, 0:NE])
            nc.scalar.copy(b2T[:, :], ps[7][:, P:P + ES]).then_inc(setup_done, 1)
            for k in range(2):
                act.sem_inc(g_free[k], 1)
                act.sem_inc(w_free[k], 1)
                act.sem_inc(st_free[k], 1)
                act.sem_inc(bias_free, 1)
                act.sem_inc(bias_free2, 1)
            act.sem_inc(y_free, 1)
            act.sem_inc(bd_used, 2)
            with act.Fori(0, TILES // 4) as i:
                act.wait_ge(zT_full, 1).then_inc(zT_full, -1)
                nc.scalar.copy(zT[:, :], ps[0][:, :]).then_inc(zT_ready, 1)
                for t in range(4):
                    act.wait_ge(g_full[t % 2], 1).then_inc(g_full[t % 2], -1)
                    act.sem_inc(bd_used, 1)
                    nc.scalar.copy(G[:, :, bass.ds((4 * i + t) * PER, PER)], ps[3 + t % 2][:, :].rearrange("p (g e) -> p e g", g=PER)).then_inc(g_free[t % 2], 1)
            act.drain().then_inc(g_done, 1)
            with act.Fori(0, NE // 2) as i:
                for k in range(2):
                    act.wait_ge(w2_full, 1).then_inc(w2_full, -1)
                    nc.scalar.copy(w2T[:, :], ps[0][:, 0:P]).then_inc(w2T_ready, 1)
                    act.wait_ge(bias_ready, 1).then_inc(bias_ready, -1)
                    act.wait_ge(h_full, 1).then_inc(h_full, -1)
                    nc.scalar.activation(h[:, :], ps[1][:, :], ACT.Relu, bias=b1e[:, k:k + 1]).then_inc(h_ready, 1)
                    act.wait_ge(r_summed, 1).then_inc(r_summed, -1)
                    act.sem_inc(w_free[k], 1)
                    act.sem_inc(bias_free, 1)
            with act.Fori(0, TILES // 2) as i:
                for k in range(2):
                    act.wait_ge(rt_full, 1).then_inc(rt_full, -1)
                    nc.scalar.copy(Rt[:, :, :], ps[3][:, :].rearrange("p (g d) -> p g d", g=PER)).then_inc(rt_ready, 1)

        @block.vector
        def _(dve):
            dve.wait_ge(iota_done, 1)
            nc.vector.tensor_scalar(tie[:, :], tie_i[:, :], 1e-6 / (GROUP - 1), None, ALU.mult).then_inc(step, 1)
            dve.wait_ge(step, 1).then_inc(step, -1)
            with dve.Fori(0, TILES // 4) as i:
                tile_stats(nc, dve, step, x, i * 4, bn, mv, stats)
            nc.vector.tensor_scalar(var[:, :], stats[:, :, 1], EPS, None, ALU.add).then_inc(step, 1)
            dve.wait_ge(step, 1).then_inc(step, -1)
            newton_rsqrt(nc.vector, dve, step, rstd[:, :], var[:, :], tmp[:, :])
            dve.wait_ge(consts, 1)
            dve.wait_ge(loaded, 64)
            with dve.Fori(0, TILES // 4) as i:
                dve.wait_ge(bd_used, 2).then_inc(bd_used, -2)
                for t in range(4):
                    one = bass.ds(i * 4 + t, 1)
                    nc.vector.tensor_copy(mv[:, t, 0:1], stats[:, one, 0])
                    ins = nc.vector.tensor_copy(mv[:, t, 1:2], rstd[:, one])
                ins.then_inc(step, 1)
                dve.wait_ge(step, 1).then_inc(step, -1)
                for t in range(4):
                    ins = nc.vector.tensor_scalar(z[:, t, :], x[:, bass.ds(i * 4 + t, 1), :], mv[:, t, 0:1], mv[:, t, 1:2], ALU.subtract, ALU.mult)
                ins.then_inc(z_ready, 1)
                dve.wait_ge(logits, 1).then_inc(logits, -1)
                nc.vector.scalar_tensor_tensor(L[:, :], ps[1][:, :], bcol[:, 0:1], tie[:, :], ALU.add, ALU.add).then_inc(step, 1)
                dve.wait_ge(step, 1).then_inc(step, -1)
                nc.vector.tensor_reduce(top[:, :], L[:, :].rearrange("p (n t) -> p n t", t=GROUP), AX.X, ALU.max).then_inc(step, 1)
                dve.wait_ge(step, 1).then_inc(step, -1)
                nc.vector.tensor_tensor(pT4[:, :, :].rearrange("p a (n t) -> p (a n) t", t=GROUP), L[:, :].rearrange("p (n t) -> p n t", t=GROUP), top[:, :].unsqueeze(2).to_broadcast([P, 16, GROUP]), ALU.is_equal).then_inc(step, 1)
                dve.wait_ge(step, 1).then_inc(step, -1)
                nc.vector.tensor_copy(permT[:, bass.ds(i * 4, 4), :], pT4[:, :, :]).then_inc(perm_ready, 1)
                dve.wait_ge(perm_full, 1).then_inc(perm_full, -1)
                for t in range(4):
                    if t >= 2:
                        dve.wait_ge(bd_used, 1).then_inc(bd_used, -1)
                    nc.vector.tensor_tensor(bd[:, t % 2, :, :], blk[:, :, :], ps[2][:, P * t:P * t + P].unsqueeze(1).to_broadcast([P, PER, P]), ALU.mult).then_inc(bd_ready, 1)
            with dve.Fori(0, NE // 2) as i:
                for k in range(2):
                    dve.wait_ge(h_ready, 1).then_inc(h_ready, -1)
                    nc.vector.tensor_tensor(hb[:, :, :], blk[:, :, :], h[:, :].rearrange("p (s n) -> p s n", s=NS), ALU.mult).then_inc(hb_ready, 1)
                    dve.wait_ge(bias_ready2, 1).then_inc(bias_ready2, -1)
                    dve.wait_ge(r_full, 1).then_inc(r_full, -1)
                    dve.sem_inc(r_summed, 1)
                    nc.vector.tensor_tensor(R[:, :, bass.ds((2 * i + k) * NS, NS)].rearrange("p n s -> p s n"), ps[2][:, :].rearrange("p (s n) -> p s n", s=NS), b2e[:, k, :].unsqueeze(2).to_broadcast([P, NS, NG]), ALU.add).then_inc(bias_free2, 1)
            dve.drain().then_inc(r_done, 1)
            with dve.Fori(0, TILES // 2) as i:
                for k in range(2):
                    dve.wait_ge(y_full, 1).then_inc(y_full, -1)
                    dve.sem_inc(st_free[k], 1)
                    tile = x[:, bass.ds(2 * i + k, 1), :]
                    nc.vector.scalar_tensor_tensor(tile, ps[4][:, 0:P].unsqueeze(1), 0.5, tile, ALU.mult, ALU.add).then_inc(y_free, 1)


def prepare_attention(nc, x, ident, dram, outs, slopes):
    gamma, w_q, w_kv, null_kv, q_scale, k_scale, w_out = dram
    xnT, wo, wqkv, scales, dist, null_dist, slope, null_keys, nvo = outs
    TILES = x.shape[1]
    HP = wo.shape[1] - 1
    HEADS, _, DH = null_kv.shape
    ROWS = HEADS * 4
    NT = null_dist.shape[1]
    NB = TILES // NT
    FAR = dist.shape[1] - P
    with ExitStack() as ctx:
        sb = lambda n, s, d=F32: ctx.enter_context(nc.sbuf_tensor("p_" + n, s, d))
        sem = lambda n: ctx.enter_context(nc.semaphore("p_" + n))
        ps = [ctx.enter_context(nc.psum_tensor(f"p_ps{k}", [P, 4 * P], F32)) for k in range(5)]
        stats = sb("stats", [P, TILES, 2])
        bn = sb("bn", [P, 4, 6])
        mv = sb("mv", [P, 4, 2])
        var = sb("var", [P, TILES])
        rstd = sb("rstd", [P, TILES])
        tmp = sb("tmp", [P, TILES])
        z = sb("z", [P, TILES, P])
        zn = sb("zn", [P, 2, 4, P])
        gcol = sb("gcol", [P, 1])
        qs = sb("qs", [P, DH])
        ks = sb("ks", [P, DH])
        qs_col = sb("qs_col", [P, 1])
        ks_col = sb("ks_col", [P, 1])
        row_scales = sb("row_scales", [P, DH])
        identr = sb("identr", [P, P], F32R)
        nk = sb("nk", [ROWS, 2, DH])
        nsq = sb("nsq", [ROWS, DH])
        ns = sb("ns", [ROWS, 1])
        nr = sb("nr", [ROWS, 1])
        nt = sb("nt", [ROWS, 1])
        nkn = sb("nkn", [ROWS, 2, DH])
        nhi = sb("nhi", [ROWS, 2, DH], F32R)
        nlo = sb("nlo", [ROWS, 2, DH], F32R)
        nvb = sb("nvb", [P, HP, 4, 4 * HP])
        blk = sb("blk", [P, 4, P])
        dist_i = sb("dist_i", [P, FAR + P], I32)
        null_dist_i = sb("null_dist_i", [P, NT, 2], I32)

        loaded = sem("loaded")
        pool_step = sem("pool_step")
        iotas = sem("iotas")
        dist_float = sem("dist_float")
        masks = sem("masks")
        step = sem("step")
        null_split = sem("null_split")
        null_full = sem("null_full")
        nvb_ready = sem("nvb_ready")
        nvo_full = sem("nvo_full")
        zn_ready = [sem(f"zn_ready{k}") for k in range(2)]
        zT_full = [sem(f"zT_full{k}") for k in range(2)]
        zn_free = [sem(f"zn_free{k}") for k in range(2)]

        block = ctx.enter_context(nc.Block("prepare"))

        @block.sync
        def _(sp):
            sp.dma_start(gcol[:, :], gamma.unsqueeze(1)).then_inc(loaded, 16)
            sp.dma_start(qs[:, :], q_scale.unsqueeze(0).to_broadcast([P, DH])).then_inc(loaded, 16)
            sp.dma_start(ks[:, :], k_scale.unsqueeze(0).to_broadcast([P, DH])).then_inc(loaded, 16)
            for k in range(2):
                sp.dma_start(nk[:, k, :], null_kv.rearrange("h c d -> (h c) d")).then_inc(loaded, 16)
            for k in range(2):
                sp.dma_start(qs_col[DH * k:DH * k + DH, :], q_scale.unsqueeze(1)).then_inc(loaded, 16)
                sp.dma_start(ks_col[DH * k:DH * k + DH, :], k_scale.unsqueeze(1)).then_inc(loaded, 16)
            sp.dma_start(wo[:, 1:HP + 1, :], w_out.rearrange("(m p) n -> p m n", p=P)).then_inc(loaded, 16)
            for part, w in enumerate((w_q, w_kv[:, 0:HP * P], w_kv[:, HP * P:2 * HP * P])):
                w = w.rearrange("p (m n) -> p m n", n=P)
                sp.dma_start(wqkv[:, 0:HP, P * part:P * part + P], w).then_inc(loaded, 16)
                sp.dma_start(wqkv[:, HP:HP + 1, P * part:P * part + P], w[:, 0:1, :]).then_inc(loaded, 16)
            sp.wait_ge(loaded, 16 * 16)

        @block.gpsimd
        def _(pool):
            nc.gpsimd.iota(dist_i[:, :], [[1, FAR + P]], base=-FAR, channel_multiplier=-1)
            nc.gpsimd.iota(null_dist_i[:, :, :], [[P, NT], [-1, 2]], base=2, channel_multiplier=1).then_inc(iotas, 1)
            nc.gpsimd.memset(blk[:, :, :], 1.0)
            nc.gpsimd.memset(nvb[:, :, :, :], 0.0)
            nc.gpsimd.memset(wo[:, 0:1, :], 0.0)
            for h, m in enumerate(slopes + slopes[0:2]):
                ins = nc.gpsimd.memset(slope[:, h:h + 1], float(m))
            ins.then_inc(pool_step, 1)
            pool.wait_ge(pool_step, 1).then_inc(pool_step, -1)
            nc.gpsimd.affine_select(out=blk[:, :, :], in_=blk[:, :, :], compare_op=ALU.is_ge, fill=0.0, base=0, pattern=[[-32, 4], [0, P]], channel_multiplier=1).then_inc(pool_step, 1)
            pool.wait_ge(pool_step, 1).then_inc(pool_step, -1)
            nc.gpsimd.affine_select(out=blk[:, :, :], in_=blk[:, :, :], compare_op=ALU.is_ge, fill=0.0, base=31, pattern=[[32, 4], [0, P]], channel_multiplier=-1).then_inc(masks, 1)
            pool.wait_ge(dist_float, 1).then_inc(dist_float, -1)
            nc.gpsimd.affine_select(out=dist[:, :], in_=dist[:, :], compare_op=ALU.is_ge, fill=-1e37, base=FAR, pattern=[[-1, FAR + P]], channel_multiplier=1).then_inc(pool_step, 1)
            pool.wait_ge(pool_step, 1)

        @block.tensor
        def _(pe):
            pe.wait_ge(null_split, 1).then_inc(null_split, -1)
            nc.tensor.transpose(ps[2][:, 0:ROWS].bitcast(F32R), nhi[:, :, :], identr[0:ROWS, 0:ROWS])
            nc.tensor.transpose(ps[2][:, P:P + ROWS].bitcast(F32R), nlo[:, :, :], identr[0:ROWS, 0:ROWS])
            nc.tensor.transpose(ps[2][:, 2 * P:2 * P + ROWS], nk[:, :, :], ident[0:ROWS, 0:ROWS]).then_inc(null_full, 1)
            pe.wait_ge(nvb_ready, 1).then_inc(nvb_ready, -1)
            for m in range(HP):
                ins = nc.tensor.matmul(ps[3][:, 0:P], nvb[:, m, :, :], wo[:, m + 1, :], start=(m == 0), stop=(m == HP - 1))
            ins.then_inc(nvo_full, 1)
            with pe.Fori(0, TILES // 8) as i:
                for k in range(2):
                    pe.wait_ge(zn_ready[k], 1).then_inc(zn_ready[k], -1)
                    for t in range(4):
                        ins = nc.tensor.transpose(ps[k][:, P * t:P * t + P], zn[:, k, t, :], ident[:, :])
                    ins.then_inc(zT_full[k], 1)

        @block.scalar
        def _(act):
            act.wait_ge(loaded, 16 * 16)
            for k in range(2):
                act.sem_inc(zn_free[k], 1)
            flat = xnT[:, :, :].rearrange("p b n -> p (b n)")
            with act.Fori(0, TILES // 8) as i:
                for k in range(2):
                    act.wait_ge(zT_full[k], 1).then_inc(zT_full[k], -1)
                    nc.scalar.activation(flat[:, bass.ds((2 * i + k) * 4 * P, 4 * P)], ps[k][:, :], ACT.Copy, scale=gcol[:, 0:1]).then_inc(zn_free[k], 1)

        @block.vector
        def _(dve):
            nc.vector.tensor_copy(identr[:, :], ident[:, :]).then_inc(step, 1)
            dve.wait_ge(step, 1).then_inc(step, -1)
            dve.wait_ge(iotas, 1)
            nc.vector.tensor_copy(dist[:, :], dist_i[:, :]).then_inc(step, 1)
            dve.wait_ge(step, 1).then_inc(step, -1)
            nc.vector.tensor_copy(null_dist[:, :, :], null_dist_i[:, :, :]).then_inc(dist_float, 1)
            dve.wait_ge(loaded, 16 * 16)
            nc.vector.scalar_tensor_tensor(scales[:, :], qs_col[:, :], 8.0, ks_col[:, :], ALU.mult, ALU.mult)
            nc.vector.scalar_tensor_tensor(row_scales[:, :], qs[:, :], 8.0, ks[:, :], ALU.mult, ALU.mult).then_inc(step, 1)
            dve.wait_ge(step, 1).then_inc(step, -1)
            nc.vector.tensor_tensor(nsq[:, :], nk[:, 0, :], nk[:, 0, :], ALU.mult).then_inc(step, 1)
            dve.wait_ge(step, 1).then_inc(step, -1)
            nc.vector.tensor_reduce(ns[:, :], nsq[:, :], AX.X, ALU.add).then_inc(step, 1)
            dve.wait_ge(step, 1).then_inc(step, -1)
            nc.vector.tensor_scalar(ns[:, :], ns[:, :], 1e-24, None, ALU.max).then_inc(step, 1)
            dve.wait_ge(step, 1).then_inc(step, -1)
            newton_rsqrt(nc.vector, dve, step, nr[:, :], ns[:, :], nt[:, :])
            nc.vector.scalar_tensor_tensor(nkn[:, :, :], nk[:, :, :], nr[:, 0:1], row_scales[0:ROWS, :].unsqueeze(1).to_broadcast([ROWS, 2, DH]), ALU.mult, ALU.mult).then_inc(step, 1)
            dve.wait_ge(step, 1).then_inc(step, -1)
            nc.vector.tensor_copy(nhi[:, :, :], nkn[:, :, :]).then_inc(step, 1)
            dve.wait_ge(step, 1).then_inc(step, -1)
            nc.vector.tensor_tensor(nlo[:, :, :], nkn[:, :, :], nhi[:, :, :].bitcast(F32), ALU.subtract).then_inc(null_split, 1)
            dve.wait_ge(null_full, 1).then_inc(null_full, -1)
            for part in range(2):
                keys = ps[2][:, P * part:P * part + ROWS].rearrange("p (h c) -> p h c", c=4)[:, :, 0:4:2]
                pairs = keys.rearrange("p (m h) c -> p m h c", h=2)
                nc.vector.tensor_copy(null_keys[:, 0:HP, part, :, :], pairs)
                nc.vector.tensor_copy(null_keys[:, HP:HP + 1, part, :, :], pairs[:, 0:1])
            dve.wait_ge(masks, 1)
            values = ps[2][:, 2 * P:2 * P + ROWS].rearrange("p (h c) -> p h c", c=4)[:, :, 1:4:2]
            for m in range(HP):
                for h in range(2):
                    ins = nc.vector.tensor_copy(nvb[DH * h:DH * h + DH, m, :, 4 * m + 2 * h:4 * m + 2 * h + 2], values[DH * h:DH * h + DH, 2 * m + h, :].unsqueeze(1).to_broadcast([DH, 4, 2]))
            ins.then_inc(nvb_ready, 1)
            dve.wait_ge(nvo_full, 1).then_inc(nvo_full, -1)
            nc.vector.tensor_tensor(nvo[:, :, :], blk[:, :, :], ps[3][:, 0:P].unsqueeze(1).to_broadcast([P, 4, P]), ALU.mult).then_inc(step, 1)
            dve.wait_ge(step, 1).then_inc(step, -1)

            def norm_columns(i, t):
                nc.vector.tensor_copy(mv[:, t, 0:1], stats[:, bass.ds(4 * i + t, 1), 0])
                return nc.vector.tensor_copy(mv[:, t, 1:2], rstd[:, bass.ds(4 * i + t, 1)])

            for src in (x, z):
                with dve.Fori(0, TILES // 4) as i:
                    tile_stats(nc, dve, step, src, i * 4, bn, mv, stats)
                nc.vector.tensor_scalar(var[:, :], stats[:, :, 1], EPS, None, ALU.add).then_inc(step, 1)
                dve.wait_ge(step, 1).then_inc(step, -1)
                newton_rsqrt(nc.vector, dve, step, rstd[:, :], var[:, :], tmp[:, :])
                if src is x:
                    with dve.Fori(0, TILES // 4) as i:
                        for t in range(4):
                            ins = norm_columns(i, t)
                        ins.then_inc(step, 1)
                        dve.wait_ge(step, 1).then_inc(step, -1)
                        for t in range(4):
                            ins = nc.vector.tensor_scalar(z[:, bass.ds(4 * i + t, 1), :], x[:, bass.ds(4 * i + t, 1), :], mv[:, t, 0:1], mv[:, t, 1:2], ALU.subtract, ALU.mult)
                        ins.then_inc(step, 1)
                        dve.wait_ge(step, 1).then_inc(step, -1)
            with dve.Fori(0, TILES // 8) as i:
                for k in range(2):
                    for t in range(4):
                        ins = norm_columns(2 * i + k, t)
                    ins.then_inc(step, 1)
                    dve.wait_ge(step, 1).then_inc(step, -1)
                    dve.wait_ge(zn_free[k], 1).then_inc(zn_free[k], -1)
                    for t in range(4):
                        ins = nc.vector.tensor_scalar(zn[:, k, t, :], z[:, bass.ds(4 * (2 * i + k) + t, 1), :], mv[:, t, 0:1], mv[:, t, 1:2], ALU.subtract, ALU.mult)
                    ins.then_inc(step, 1)
                    dve.wait_ge(step, 1).then_inc(step, -1)
                    dve.sem_inc(zn_ready[k], 1)


def attention(nc, x, ident, dram):
    gamma, w_q, w_kv, null_kv, q_scale, k_scale, w_out = dram
    HEADS, NULL, DH = null_kv.shape[0], null_kv.shape[1] // 2, null_kv.shape[2]
    NB = 4
    HP = HEADS // 2
    NT = x.shape[1] // NB
    N = NT * P
    FAR = N
    QK = 2 * P
    start = 2.0 ** (-2.0 ** (-(4 - 3.0)))
    slopes = [start * start ** i for i in range(HEADS)]
    RING = 3
    with ExitStack() as ctx:
        sb = lambda n, s, d=F32: ctx.enter_context(nc.sbuf_tensor("a_" + n, s, d))
        sem = lambda n: ctx.enter_context(nc.semaphore("a_" + n))

        xnT = sb("xnT", [P, NB, N])
        wo = sb("wo", [P, HP + 1, P])
        wqkv = sb("wqkv", [P, HP + 1, 3 * P])
        scales = sb("scales", [P, 1])
        dist = sb("dist", [P, FAR + P])
        null_dist = sb("null_dist", [P, NT, NULL])
        slope = sb("slope", [P, HEADS + 2])
        null_keys = sb("null_keys", [P, HP + 1, 2, 2, NULL], F32R)
        nvo = sb("nvo", [P, 4, P])

        prepare_attention(nc, x, ident, dram, (xnT, wo, wqkv, scales, dist, null_dist, slope, null_keys, nvo), slopes)

        qT = [sb(f"qT{r}", [P, 2, N], F32R) for r in range(2)]
        khT = [sb(f"khT{r}", [P, 2, N], F32R) for r in range(2)]
        klT = [sb(f"klT{r}", [P, 2, N], F32R) for r in range(2)]
        qkv = [sb(f"qkv{r}", [P, NT, 3 * P]) for r in range(2)]
        null_neg = [sb(f"null_neg{r}", [P, NT, 2, NULL]) for r in range(2)]
        null_min = [sb(f"null_min{r}", [P, NT, 2]) for r in range(2)]
        w_now = sb("w_now", [P, 3 * P])
        null_now = sb("null_now", [P, 2, 2, NULL], F32R)
        slope_now = sb("slope_now", [P, 2])
        table = sb("table", [P, 2, FAR + P])
        square = sb("square", [P, NT // 2, 4, DH])
        norm2 = sb("norm2", [P, NT // 2, 4])
        rnorm = sb("rnorm", [P, NT // 2, 4])
        ntmp = sb("ntmp", [P, NT // 2, 4])
        prob = [sb(f"prob{k}", [P, 2, N]) for k in range(2)]
        probT = [sb(f"probT{k}", [P, 2, N]) for k in range(2)]
        neg_max = sb("neg_max", [P, NT, 2])
        row_sum = sb("row_sum", [P, NT, 2])
        null_arg = sb("null_arg", [P, NT // 2, 2, NULL])
        null_prob = sb("null_prob", [P, NT // 2, 2, NULL])
        total = sb("total", [P, NT // 2, 2])
        rtotal = sb("rtotal", [P, NT // 2, 2])
        rtotal_wide = sb("rtotal_wide", [P, NT // 2, 2, DH])
        null_all = sb("null_all", [P, NB, NT, 4 * HP])
        oT = sb("oT", [P, 4 * P])
        nullT = oT[:, 0:P]

        score = [ctx.enter_context(nc.psum_tensor(f"a_score{h}", [P, N], F32)) for h in range(2)]
        ring = [ctx.enter_context(nc.psum_tensor(f"a_ring{k}", [P, 4 * P], F32)) for k in range(RING)]
        outT = ctx.enter_context(nc.psum_tensor("a_outT", [P, 4 * P], F32))

        step = sem("step")
        pool_step = sem("pool_step")
        zeroed = sem("zeroed")
        score_full = [sem(f"score_full{h}") for h in range(2)]
        score_free = [sem(f"score_free{h}") for h in range(2)]
        shifted = [sem(f"shifted{h}") for h in range(2)]
        prob_ready = [sem(f"prob_ready{h}") for h in range(2)]
        to_act = [sem(f"to_act{k}") for k in range(RING)]
        to_dve = [sem(f"to_dve{k}") for k in range(RING)]
        freed = [sem(f"freed{k}") for k in range(RING)]
        high_ready = sem("high_ready")
        o_full = sem("o_full")
        o_copied = sem("o_copied")
        null_arg_ready = sem("null_arg_ready")
        null_prob_ready = sem("null_prob_ready")
        rtotal_ready = sem("rtotal_ready")
        projected = sem("projected")
        squared = sem("squared")
        summed = sem("summed")
        normed = sem("normed")
        w_free = sem("w_free")
        w_loaded = sem("w_loaded")
        null_loaded = sem("null_loaded")
        nullT_ready = sem("nullT_ready")

        extra = {
            0: [("PV", 7), ("O", 1), ("PROJ", 0), ("RB", 1), ("PROJ", 1), ("PROJ", 2), ("PROJ", 3), ("SQ", 0)],
            1: [("Y", 1), ("PROJ", 4), ("PROJ", 5), ("PV", 0), ("RS", 0), ("NM", 0)],
            2: [("PROJ", 6), ("PV", 1), ("PROJ", 7), ("SQ", 1)],
            3: [("R2", 0), ("C", 0, 0), ("PV", 2), ("C", 0, 1), ("C", 0, 2), ("RS", 1), ("NM", 1)],
            4: [("PV", 3), ("O", 0), ("C", 0, 3), ("RB", 0)],
            5: [("Y", 0), ("SLOPE",), ("NULL", 0), ("PV", 4), ("C", 1, 0)],
            6: [("C", 1, 1), ("PV", 5), ("C", 1, 2)],
            7: [("R2", 1), ("C", 1, 3), ("PV", 6), ("NULL", 1)],
        }
        plan = []
        for t in range(NT):
            u = (t + 1) % NT
            plan += [("S", u, 0), ("T", t, 0), ("S", u, 1)]
            for h in range(2):
                plan += [("TAB", h)] * (u == 0) + [("SM", u, h)] + [("T", t, 1)] * (h == 0) + [("R1", t // 4)] * (h == 0 and t % 4 == 3)
            plan += extra[t]
        bank, fills = {}, 0
        for s in plan:
            for g in range(1 + (s[0] == "T" and s[1] >= 4)):
                if s[0] in ("T", "C", "PROJ", "NULL", "RB", "Y"):
                    bank[s, g] = fills % RING
                    fills += 1
        first = [s for s in plan if s[0] in ("PROJ", "SQ", "RS", "NM", "C", "NULL", "SLOPE", "TAB") or s[0] in ("S", "SM") and s[1] == 0]
        rest = [("PV", 7), ("O", 1), ("RB", 1), ("Y", 1)]

        def turns(eng, run):
            run(first, -1, NB - 1)
            with eng.Fori(0, HP) as hp:
                for b in range(NB):
                    run(plan, hp, b)
            run(rest, HP, 0)

        block = ctx.enter_context(nc.Block("attention"))

        @block.sync
        def _(sp):
            sp.dma_start(w_now[:, :].unsqueeze(1), wqkv[:, 0:1, :]).then_inc(w_loaded, 16)
            with sp.Fori(0, HP) as hp:
                sp.wait_ge(w_free, 1).then_inc(w_free, -1)
                sp.dma_start(w_now[:, :].unsqueeze(1), wqkv[:, bass.ds(hp + 1, 1), :]).then_inc(w_loaded, 16)

        @block.gpsimd
        def _(pool):
            def run(steps, hp, b):
                for s in steps:
                    if s[0] in ("SQ", "NM"):
                        four = slice(4 * s[1], 4 * s[1] + 4)
                        qk = qkv[(b + 1) % 2][:, four, 0:QK]
                    if s[0] == "SQ":
                        pool.wait_ge(projected, 1).then_inc(projected, -1)
                        nc.gpsimd.tensor_tensor(square[:, :, :, :].rearrange("p t v d -> p t (v d)"), qk, qk, ALU.mult).then_inc(squared, 1)
                    if s[0] == "NM":
                        pool.wait_ge(summed, 1).then_inc(summed, -1)
                        newton_rsqrt(nc.gpsimd, pool, pool_step, rnorm[:, :, :], norm2[:, :, :], ntmp[:, :, :])
                        vectors = qk.rearrange("p t (v d) -> p t v d", d=DH)
                        nc.gpsimd.tensor_tensor(vectors, vectors, rnorm[:, :, :].unsqueeze(3).to_broadcast([P, 4, 4, DH]), ALU.mult).then_inc(normed, 1)

            nc.gpsimd.memset(qkv[1][:, :, :], 0.0)
            nc.gpsimd.memset(probT[1][:, :, :], 0.0)
            nc.gpsimd.memset(rtotal_wide[:, :, :, :], 0.0).then_inc(zeroed, 1)
            turns(pool, run)

        @block.tensor
        def _(pe):
            def run(steps, hp, b):
                r, n = b % 2, (b + 1) % 2
                for s in steps:
                    if s[0] == "S":
                        _, t, h = s
                        q = r if t else n
                        pe.wait_ge(score_free[h], 1).then_inc(score_free[h], -1)
                        for c in range(0, P * (t + 1), 4 * P):
                            e = min(c + 4 * P, P * (t + 1))
                            nc.tensor.matmul(score[h][:, c:e], qT[q][:, h, P * t:P * t + P], khT[q][:, h, c:e], start=True, stop=False)
                            ins = nc.tensor.matmul(score[h][:, c:e], qT[q][:, h, P * t:P * t + P], klT[q][:, h, c:e], start=False, stop=True)
                        ins.then_inc(score_full[h], 1)
                    if s[0] == "T":
                        _, t, h = s
                        pe.wait_ge(prob_ready[h], 1).then_inc(prob_ready[h], -1)
                        for g in range(1 + (t >= 4)):
                            k = bank[s, g]
                            pe.wait_ge(freed[k], 1).then_inc(freed[k], -1)
                            for j in range(4 * g, min(4 * g + 4, t + 1)):
                                ins = nc.tensor.transpose(ring[k][:, P * (j % 4):P * (j % 4) + P], prob[t % 2][:, h, P * j:P * j + P], ident[:, :])
                            ins.then_inc((to_act, to_dve)[h][k], 1)
                    if s[0] == "PV":
                        t = s[1]
                        v = qkv[n if t == 7 else r]
                        if steps is rest:
                            for k in range(RING):
                                pe.wait_ge(freed[k], 1)
                        for j in range(t + 1):
                            for h in range(2):
                                ins = nc.tensor.matmul(outT[DH * h:DH * h + DH, P * (t % 4):P * (t % 4) + P], v[:, j, QK + DH * h:QK + DH * h + DH], probT[t % 2][:, h, P * j:P * j + P], start=(j == 0), stop=(j == t))
                        if t % 4 == 3:
                            ins.then_inc(o_full, 1)
                    if s[0] == "RB":
                        k = bank[s, 0]
                        pe.wait_ge(rtotal_ready, 1).then_inc(rtotal_ready, -1)
                        pe.wait_ge(freed[k], 1).then_inc(freed[k], -1)
                        for t in range(4):
                            ins = nc.tensor.transpose(ring[k][:, P * t:P * t + P], rtotal_wide[:, t, :, :], ident[:, :])
                        ins.then_inc(to_dve[k], 1)
                    if s[0] == "Y":
                        k = bank[s, 0]
                        if steps is rest:
                            pe.wait_ge(freed[bank[("RB", 1), 0]], 1)
                        pe.wait_ge(freed[k], 1).then_inc(freed[k], -1)
                        pair = hp + 1 if s[1] == 0 or b > 0 else hp
                        for t in range(4):
                            ins = nc.tensor.matmul(ring[k][:, P * t:P * t + P], oT[:, P * t:P * t + P], wo[:, bass.ds(pair, 1), :], start=True, stop=True)
                        ins.then_inc(to_dve[k], 1)
                    if s[0] == "PROJ":
                        t = s[1]
                        k = bank[s, 0]
                        if t == 0 and b == NB - 1:
                            pe.wait_ge(w_loaded, 16).then_inc(w_loaded, -16)
                        pe.wait_ge(freed[k], 1).then_inc(freed[k], -1)
                        nc.tensor.matmul(ring[k][:, 0:3 * P], xnT[:, (b + 1) % NB, P * t:P * t + P], w_now[:, :], start=True, stop=True).then_inc(to_act[k], 1)
                    if s[0] == "C":
                        _, g, vec = s
                        k = bank[s, 0]
                        if vec == 0:
                            pe.wait_ge(normed, 1).then_inc(normed, -1)
                        pe.wait_ge(freed[k], 1).then_inc(freed[k], -1)
                        for t in range(4):
                            for half in (0, DH):
                                ins = nc.tensor.matmul(ring[k][half:half + DH, P * t:P * t + P], qkv[n][:, 4 * g + t, DH * vec:DH * vec + DH], ident[:, :], start=True, stop=True)
                        ins.then_inc(to_act[k], 1)
                    if s[0] == "NULL":
                        g = s[1]
                        k = bank[s, 0]
                        if g == 0 and b == NB - 1:
                            pe.wait_ge(null_loaded, 1).then_inc(null_loaded, -1)
                        pe.wait_ge(freed[k], 1).then_inc(freed[k], -1)
                        for t in range(4):
                            for h in range(2):
                                o = ring[k][:, 4 * t + 2 * h:4 * t + 2 * h + 2]
                                query = qT[n][:, h, P * (4 * g + t):P * (4 * g + t) + P]
                                nc.tensor.matmul(o, query, null_now[:, 0, h, :], start=True, stop=False)
                                ins = nc.tensor.matmul(o, query, null_now[:, 1, h, :], start=False, stop=True)
                        ins.then_inc(to_dve[k], 1)

            for k in range(RING):
                pe.sem_inc(freed[k], 1)
            for h in range(2):
                pe.sem_inc(score_free[h], 1)
            pe.wait_ge(zeroed, 2)
            pe.sem_inc(rtotal_ready, 1)
            turns(pe, run)
            for k in range(RING):
                pe.wait_ge(freed[k], 1)
            for b in range(NB):
                for g in range(2):
                    nc.tensor.transpose(ring[0][:, 0:P], null_all[:, b, 4 * g:4 * g + 4, :], ident[:, :]).then_inc(to_act[0], 1)
                    pe.wait_ge(nullT_ready, 1).then_inc(nullT_ready, -1)
                    pe.wait_ge(freed[1], 1).then_inc(freed[1], -1)
                    nc.tensor.matmul(ring[1][:, :], nullT, nvo[:, :, :], start=True, stop=True).then_inc(to_dve[1], 1)

        @block.scalar
        def _(act):
            def run(steps, hp, b):
                n = (b + 1) % 2
                for s in steps:
                    if s[0] == "T" and s[2] == 0:
                        t = s[1]
                        for g in range(1 + (t >= 4)):
                            k = bank[s, g]
                            c, e = 4 * P * g, min(4 * P * (g + 1), P * (t + 1))
                            act.wait_ge(to_act[k], 1).then_inc(to_act[k], -1)
                            nc.scalar.copy(probT[t % 2][:, 0, c:e], ring[k][:, 0:e - c]).then_inc(freed[k], 1)
                    if s[0] == "SM":
                        _, t, h = s
                        p = prob[t % 2][:, h, 0:P * (t + 1)]
                        act.wait_ge(shifted[h], 1).then_inc(shifted[h], -1)
                        act.sem_inc(score_free[h], 1)
                        nc.scalar.activation(p, p, ACT.Exp, bias=neg_max[:, t, h:h + 1], scale=-1.0, accum_out=row_sum[:, t, h:h + 1]).then_inc(prob_ready[h], 1)
                    if s[0] == "R1":
                        act.wait_ge(null_arg_ready, 1).then_inc(null_arg_ready, -1)
                        nc.scalar.activation(null_prob[:, :, :, :], null_arg[:, :, :, :], ACT.Exp).then_inc(null_prob_ready, 1)
                    if s[0] == "O":
                        act.wait_ge(o_full, 1).then_inc(o_full, -1)
                        nc.scalar.copy(oT[:, :], outT[:, :]).then_inc(o_copied, 1)
                    if s[0] == "PROJ":
                        k = bank[s, 0]
                        act.wait_ge(to_act[k], 1).then_inc(to_act[k], -1)
                        if s[1] % 4 == 3:
                            nc.scalar.copy(qkv[n][:, s[1], 0:QK], ring[k][:, 0:QK]).then_inc(projected, 1)
                            nc.scalar.copy(qkv[n][:, s[1], QK:3 * P], ring[k][:, QK:3 * P]).then_inc(freed[k], 1)
                        else:
                            nc.scalar.copy(qkv[n][:, s[1], :], ring[k][:, 0:3 * P]).then_inc(freed[k], 1)
                        if s[1] == NT - 1 and b == NB - 2:
                            act.sem_inc(w_free, 1)
                    if s[0] == "C":
                        _, g, vec = s
                        k = bank[s, 0]
                        act.wait_ge(to_act[k], 1).then_inc(to_act[k], -1)
                        high = (qT, khT)[vec // 2][n][:, vec % 2, 4 * P * g:4 * P * g + 4 * P]
                        nc.scalar.activation(high, ring[k][:, :], ACT.Copy, scale=1.0 if vec < 2 else scales[:, 0:1]).then_inc(high_ready, 1)

            turns(act, run)
            for b in range(NB):
                for g in range(2):
                    act.wait_ge(to_act[0], 1).then_inc(to_act[0], -1)
                    nc.scalar.copy(nullT, ring[0][:, 0:P]).then_inc(nullT_ready, 1)

        @block.vector
        def _(dve):
            def run(steps, hp, b):
                r, n = b % 2, (b + 1) % 2
                for s in steps:
                    if s[0] == "T" and s[2] == 1:
                        t = s[1]
                        for g in range(1 + (t >= 4)):
                            k = bank[s, g]
                            c, e = 4 * P * g, min(4 * P * (g + 1), P * (t + 1))
                            dve.wait_ge(to_dve[k], 1).then_inc(to_dve[k], -1)
                            nc.vector.tensor_copy(probT[t % 2][:, 1, c:e], ring[k][:, 0:e - c]).then_inc(freed[k], 1)
                    if s[0] == "SM":
                        _, t, h = s
                        w, q = P * (t + 1), r if t else n
                        dve.wait_ge(score_full[h], 1).then_inc(score_full[h], -1)
                        nc.vector.tensor_tensor_reduce(out=prob[t % 2][:, h, 0:w], in0=score[h][:, 0:w], in1=table[:, h, FAR - P * t:FAR + P], scale=-1.0, scalar=null_min[q][:, t, h:h + 1], op0=ALU.add, op1=ALU.min, accum_out=neg_max[:, t, h:h + 1]).then_inc(shifted[h], 1)
                    if s[0] == "R1":
                        g = 4 * s[1]
                        nc.vector.tensor_tensor(null_arg[:, :, :, :], neg_max[:, g:g + 4, :].unsqueeze(3).to_broadcast([P, 4, 2, NULL]), null_neg[r][:, g:g + 4, :, :], ALU.subtract).then_inc(null_arg_ready, 1)
                    if s[0] == "R2":
                        g = 4 * s[1]
                        dve.wait_ge(null_prob_ready, 1).then_inc(null_prob_ready, -1)
                        nc.vector.tensor_reduce(total[:, :, :], null_prob[:, :, :, :], AX.X, ALU.add).then_inc(step, 1)
                        dve.wait_ge(step, 1).then_inc(step, -1)
                        nc.vector.tensor_tensor(total[:, :, :], total[:, :, :], row_sum[:, g:g + 4, :], ALU.add).then_inc(step, 1)
                        dve.wait_ge(step, 1).then_inc(step, -1)
                        nc.vector.reciprocal(rtotal[:, :, :], total[:, :, :]).then_inc(step, 1)
                        dve.wait_ge(step, 1).then_inc(step, -1)
                        nc.vector.tensor_copy(rtotal_wide[:, :, :, :], rtotal[:, :, :].unsqueeze(3).to_broadcast([P, 4, 2, DH]))
                        nc.vector.tensor_tensor(null_all[:, b:b + 1, g:g + 4, bass.ds(4 * hp, 4)].rearrange("p a t (h c) -> p (a t) h c", h=2), null_prob[:, :, :, :], rtotal[:, :, :].unsqueeze(3).to_broadcast([P, 4, 2, NULL]), ALU.mult).then_inc(rtotal_ready, 1)
                    if s[0] == "RB":
                        k = bank[s, 0]
                        dve.wait_ge(to_dve[k], 1).then_inc(to_dve[k], -1)
                        dve.wait_ge(o_copied, 1).then_inc(o_copied, -1)
                        nc.vector.tensor_tensor(oT[:, :], oT[:, :], ring[k][:, :], ALU.mult).then_inc(freed[k], 1)
                    if s[0] == "Y":
                        k = bank[s, 0]
                        batch = b if s[1] == 0 else (b - 1) % NB
                        dve.wait_ge(to_dve[k], 1).then_inc(to_dve[k], -1)
                        tiles = x[:, batch * NT + 4 * s[1]:batch * NT + 4 * s[1] + 4, :]
                        nc.vector.tensor_tensor(tiles, tiles, ring[k][:, :].rearrange("p (t d) -> p t d", t=4), ALU.add).then_inc(freed[k], 1)
                    if s[0] == "RS":
                        dve.wait_ge(squared, 1).then_inc(squared, -1)
                        nc.vector.tensor_reduce(norm2[:, :, :], square[:, :, :, :], AX.X, ALU.add).then_inc(step, 1)
                        dve.wait_ge(step, 1).then_inc(step, -1)
                        nc.vector.tensor_scalar(norm2[:, :, :], norm2[:, :, :], 1e-24, None, ALU.max).then_inc(summed, 1)
                    if s[0] == "C":
                        _, g, vec = s
                        k = bank[s, 0]
                        c = slice(4 * P * g, 4 * P * g + 4 * P)
                        dve.wait_ge(high_ready, 1).then_inc(high_ready, -1)
                        if vec < 2:
                            nc.vector.tensor_tensor(qT[n][DH:P, vec, c], ring[k][DH:P, :], qT[n][DH:P, vec, c].bitcast(F32), ALU.subtract).then_inc(freed[k], 1)
                        else:
                            nc.vector.scalar_tensor_tensor(klT[n][:, vec - 2, c], ring[k][:, :], scales[:, 0:1], khT[n][:, vec - 2, c].bitcast(F32), ALU.mult, ALU.subtract).then_inc(freed[k], 1)
                    if s[0] == "SLOPE" and b == NB - 1:
                        nc.vector.tensor_copy(null_now[:, :, :, :].unsqueeze(1), null_keys[:, bass.ds(hp + 1, 1), :, :, :].bitcast(F32)).then_inc(null_loaded, 1)
                        nc.vector.tensor_copy(slope_now[:, :], slope[:, bass.ds(2 * (hp + 1), 2)]).then_inc(step, 1)
                        dve.wait_ge(step, 1).then_inc(step, -1)
                    if s[0] == "TAB" and b == NB - 1:
                        nc.vector.tensor_scalar(table[:, s[1], :], dist[:, :], slope_now[:, s[1]:s[1] + 1], None, ALU.mult).then_inc(step, 1)
                        dve.wait_ge(step, 1).then_inc(step, -1)
                    if s[0] == "NULL":
                        k = bank[s, 0]
                        g = slice(4 * s[1], 4 * s[1] + 4)
                        dve.wait_ge(to_dve[k], 1).then_inc(to_dve[k], -1)
                        o = ring[k][:, 0:4 * 4].rearrange("p (t h c) -> p t h c", h=2, c=NULL)
                        for h in range(2):
                            ins = nc.vector.scalar_tensor_tensor(null_neg[n][:, g, h, :], null_dist[:, g, :], slope_now[:, h:h + 1], o[:, :, h, :], ALU.mult, ALU.subtract)
                        ins.then_inc(step, 1)
                        dve.wait_ge(step, 1).then_inc(step, -1)
                        nc.vector.tensor_reduce(null_min[n][:, g, :], null_neg[n][:, g, :, :], AX.X, ALU.min).then_inc(step, 1)
                        dve.wait_ge(step, 1).then_inc(step, -1)
                        dve.sem_inc(freed[k], 1)

            nc.vector.memset(outT[:, :], 0.0).then_inc(zeroed, 1)
            turns(dve, run)
            for b in range(NB):
                for g in range(2):
                    dve.wait_ge(to_dve[1], 1).then_inc(to_dve[1], -1)
                    tiles = x[:, b * NT + 4 * g:b * NT + 4 * g + 4, :]
                    nc.vector.tensor_tensor(tiles, tiles, ring[1][:, :].rearrange("p (t d) -> p t d", t=4), ALU.add).then_inc(freed[1], 1)


def build(nc, args, out):
    (x_d, gamma, w_q, w_kv, null_kv, q_scale, k_scale, w_out, Wc, bc, W1, b1, W2, b2) = args
    with ExitStack() as ctx:
        sb = lambda n, s, d=F32: ctx.enter_context(nc.sbuf_tensor(n, s, d))
        sem = lambda n: ctx.enter_context(nc.semaphore(n))
        x = sb("x", [P, 32, P])
        ident = sb("ident", [P, P])
        x_loaded = sem("x_loaded")
        ident_zero = sem("ident_zero")
        ident_made = sem("ident_made")
        stored = sem("stored")
        xv = x_d.rearrange("b (t p) d -> p (b t) d", p=P)
        ov = out.rearrange("b (t p) d -> p (b t) d", p=P)
        with nc.Block("start") as block:
            @block.sync
            def _(sp):
                sp.dma_start(x[:, :, :], xv).then_inc(x_loaded, 16)
                sp.wait_ge(x_loaded, 16)

            @block.gpsimd
            def _(pool):
                nc.gpsimd.memset(ident[:, :], 0.0).then_inc(ident_zero, 1)
                pool.wait_ge(ident_zero, 1)
                nc.gpsimd.affine_select(out=ident[:, :], in_=ident[:, :], compare_op=ALU.not_equal, fill=1.0, base=0, pattern=[[-1, P]], channel_multiplier=1).then_inc(ident_made, 1)
                pool.wait_ge(ident_made, 1)
        ffn(nc, x, ident, (Wc, bc, W1, b1, W2, b2), "f1_")
        attention(nc, x, ident, (gamma, w_q, w_kv, null_kv, q_scale, k_scale, w_out))
        ffn(nc, x, ident, (Wc, bc, W1, b1, W2, b2), "f2_")
        with nc.Block("end") as block:
            @block.sync
            def _(sp):
                sp.dma_start(ov, x[:, :, :]).then_inc(stored, 16)
                sp.wait_ge(stored, 16)


_INS = ['L0_attn_x', 'L0_attn_gamma', 'L0_attn_w_q', 'L0_attn_w_kv', 'L0_attn_null_kv', 'L0_attn_q_scale',
        'L0_attn_k_scale', 'L0_attn_w_out', 'L0_ffn_Wc', 'L0_ffn_bc', 'L0_ffn_W1', 'L0_ffn_b1', 'L0_ffn_W2', 'L0_ffn_b2']


def kernel(**inputs):
    import numpy as np
    import concourse.bacc as bacc
    from concourse.bass_utils import run_bass_kernel_spmd

    nc = bacc.Bacc("TRN2", target_bir_lowering=False, num_devices=1)
    arrays, args = {}, []
    for name in _INS:
        a = np.ascontiguousarray(inputs[name])
        arrays[f"in_{name}"] = a
        args.append(nc.dram_tensor(f"in_{name}", a.shape, mybir.dt.from_np(a.dtype), kind="ExternalInput").ap())
    out = nc.dram_tensor("out_x", inputs['L0_attn_x'].shape, F32, kind="ExternalOutput").ap()
    build(nc, args, out)
    r = run_bass_kernel_spmd(nc, [arrays], core_ids=[0])
    return r.results[0]["out_x"]
```

```python
from contextlib import ExitStack

import concourse.bass as bass
from concourse import mybir

F32 = mybir.dt.float32
F32R = mybir.dt.float32r
I32 = mybir.dt.int32
ALU = mybir.AluOpType
ACT = mybir.ActivationFunctionType
AX = mybir.AxisListType
P = 128
EPS = 1e-5


def newton_rsqrt(ops, eng, step, out, v, tmp):
    bits = out.bitcast(I32)
    ops.tensor_scalar(bits, v.bitcast(I32), -0.5, float(0x5F3759DF), ALU.mult, ALU.add).then_inc(step, 1)
    eng.wait_ge(step, 1).then_inc(step, -1)
    for _ in range(3):
        ops.tensor_tensor(tmp, out, out, ALU.mult).then_inc(step, 1)
        eng.wait_ge(step, 1).then_inc(step, -1)
        ops.tensor_tensor(tmp, tmp, v, ALU.mult).then_inc(step, 1)
        eng.wait_ge(step, 1).then_inc(step, -1)
        ops.tensor_scalar(tmp, tmp, -0.5, 1.5, ALU.mult, ALU.add).then_inc(step, 1)
        eng.wait_ge(step, 1).then_inc(step, -1)
        ops.tensor_tensor(out, tmp, out, ALU.mult).then_inc(step, 1)
        eng.wait_ge(step, 1).then_inc(step, -1)


def tile_stats(nc, dve, step, src, first, bn, mv, mean, var):
    for k in range(8):
        ins = nc.vector.bn_stats(bn[:, k, :], src[:, bass.ds(first + k, 1), :])
    ins.then_inc(step, 1)
    dve.wait_ge(step, 1).then_inc(step, -1)
    for k in range(8):
        ins = nc.vector.bn_aggr(mv[:, k, :], bn[:, k, :])
    ins.then_inc(step, 1)
    dve.wait_ge(step, 1).then_inc(step, -1)
    nc.vector.tensor_copy(mean[:, bass.ds(first, 8)], mv[:, :, 0])
    nc.vector.tensor_scalar(var[:, bass.ds(first, 8)], mv[:, :, 1], EPS, None, ALU.add).then_inc(step, 1)
    dve.wait_ge(step, 1).then_inc(step, -1)


def ffn(nc, x, ident, dram, pre):
    Wc, bc, W1, b1, W2, b2 = dram
    NE, NS, D, F = W1.shape
    ES = NE * NS
    TILES = x.shape[1]
    GROUP = 32
    PER = P // GROUP
    NG = TILES * PER
    with ExitStack() as ctx:
        sb = lambda n, s, d=F32: ctx.enter_context(nc.sbuf_tensor(pre + n, s, d))
        pb = lambda n: ctx.enter_context(nc.psum_tensor(pre + n, [P, 4 * P], F32))
        signals = []

        def sem(n):
            signals.append(nc.alloc_semaphore(pre + n))
            return signals[-1]


        G = sb("G", [P, ES, NG])
        R = sb("R", [P, NG, ES])
        permT = sb("permT", [P, TILES, P])
        bn = sb("bn", [P, 8, 6])
        mv = sb("mv", [P, 8, 2])
        mean = sb("mean", [P, TILES])
        var = sb("var", [P, TILES])
        rstd = sb("rstd", [P, TILES])
        tmp = sb("tmp", [P, TILES])
        wc = sb("wc", [P, ES])
        bcol = sb("bcol", [P, 1])
        tie = sb("tie", [P, 4 * P])
        tie_i = sb("tie_i", [P, 4 * P], I32)
        b1r = sb("b1r", [NE, NS * F])
        b2r = sb("b2r", [ES, P])
        b1T = sb("b1T", [P, NE])
        b2T = sb("b2T", [P, ES])
        z = [sb(f"z{k}", [P, 4, P]) for k in range(2)]
        zT = sb("zT", [P, 4 * P])
        L = sb("L", [P, 4 * P])
        top = sb("top", [P, 16])
        pT4 = sb("pT4", [P, 4, P])

        ps = [pb(f"ps{i}") for i in range(8)]

        loaded = sem("loaded")
        iota_done = sem("iota_done")
        step = sem("step")
        pool_step = sem("pool_step")
        rstd_ready = sem("rstd_ready")
        setup_full = sem("setup_full")
        setup_done = sem("setup_done")
        z_ready = [sem(f"z_ready{k}") for k in range(2)]
        z_split = sem("z_split")
        z_free = [sem(f"z_free{k}") for k in range(2)]
        zT_full = sem("zT_full")
        zT_ready = sem("zT_ready")
        logits = sem("logits")
        perm_ready = sem("perm_ready")
        perm_full = sem("perm_full")
        taken_ready = [sem(f"taken_ready{k}") for k in range(2)]
        g_full = [sem(f"g_full{g}") for g in range(PER)]
        g_free = [sem(f"g_free{g}") for g in range(PER)]

        with ExitStack() as select:
            sb1 = lambda n, s, d=F32: select.enter_context(nc.sbuf_tensor(pre + n, s, d))
            zh = [sb1(f"zh{k}", [P, 4, P], F32R) for k in range(2)]
            zl = [sb1(f"zl{k}", [P, 4, P], F32R) for k in range(2)]
            taken = [sb1(f"taken{k}", [P, 4, P], F32R) for k in range(2)]
            block = select.enter_context(nc.Block(pre + "select"))

            @block.sync
            def _(sp):
                sp.dma_start(wc[:, :], Wc.rearrange("d e s -> d (e s)")).then_inc(loaded, 16)
                sp.dma_start(bcol[:, :], bc.rearrange("e s -> (e s)").unsqueeze(1)).then_inc(loaded, 16)
                sp.dma_start(b1r[:, :], b1.rearrange("e s f -> e (s f)")).then_inc(loaded, 16)
                sp.dma_start(b2r[:, :], b2.rearrange("e s d -> (e s) d")).then_inc(loaded, 16)

            @block.gpsimd
            def _(pool):
                nc.gpsimd.iota(tie_i[:, :], [[0, 16], [1, GROUP]], base=0, channel_multiplier=0).then_inc(iota_done, 1)
                pool.wait_ge(rstd_ready, 1)
                with pool.Fori(0, TILES // 8) as i:
                    for k in range(2):
                        four = bass.ds(8 * i + 4 * k, 4)
                        pool.wait_ge(z_free[k], 1).then_inc(z_free[k], -1)
                        nc.gpsimd.tensor_tensor(z[k][:, :, :], x[:, four, :], mean[:, four].unsqueeze(2).to_broadcast([P, 4, P]), ALU.subtract).then_inc(pool_step, 1)
                        pool.wait_ge(pool_step, 1).then_inc(pool_step, -1)
                        nc.gpsimd.tensor_tensor(z[k][:, :, :], z[k][:, :, :], rstd[:, four].unsqueeze(2).to_broadcast([P, 4, P]), ALU.mult).then_inc(z_ready[k], 1)

            @block.tensor
            def _(pe):
                pe.wait_ge(loaded, 64)
                nc.tensor.transpose(ps[7][:, 0:NE], b1r[:, :], ident[0:NE, 0:NE])
                nc.tensor.transpose(ps[7][:, P:P + ES], b2r[:, :], ident[:, :]).then_inc(setup_full, 1)

                def gather(k, first):
                    if first == 0:
                        pe.wait_ge(taken_ready[k], 1).then_inc(taken_ready[k], -1)
                    for t in (first, first + 1):
                        for g in range(PER):
                            rows = slice(GROUP * g, GROUP * g + GROUP)
                            out = ps[3 + g][:, P * t:P * t + P]
                            if t == 0:
                                pe.wait_ge(g_free[g], 1).then_inc(g_free[g], -1)
                            nc.tensor.matmul(out, zh[k][rows, t, :], taken[k][rows, t, :], start=True, stop=False)
                            ins = nc.tensor.matmul(out, zl[k][rows, t, :], taken[k][rows, t, :], start=False, stop=True)
                            if t == 3:
                                ins.then_inc(g_full[g], 1)

                def select(k, taking):
                    pe.wait_ge(z_split, 1).then_inc(z_split, -1)
                    for t in range(4):
                        ins = nc.tensor.transpose(ps[0][:, P * t:P * t + P], z[k][:, t, :], ident[:, :])
                    ins.then_inc(zT_full, 1)
                    if taking:
                        gather(1 - k, 0)
                    pe.wait_ge(zT_ready, 1).then_inc(zT_ready, -1)
                    nc.tensor.matmul(ps[1][:, :], wc[:, :], zT[:, :], start=True, stop=True).then_inc(logits, 1)
                    if taking:
                        gather(1 - k, 2)
                    pe.wait_ge(perm_ready, 1).then_inc(perm_ready, -1)
                    for t in range(4):
                        ins = nc.tensor.transpose(ps[2][:, P * t:P * t + P], pT4[:, t, :], ident[:, :])
                    ins.then_inc(perm_full, 1)

                select(0, False)
                with pe.Fori(0, TILES // 8 - 1) as i:
                    for k in range(2):
                        select(1 - k, True)
                select(1, True)
                gather(1, 0)
                gather(1, 2)

            @block.scalar
            def _(act):
                act.wait_ge(setup_full, 1)
                nc.scalar.copy(b1T[:, :], ps[7][:, 0:NE])
                nc.scalar.copy(b2T[:, :], ps[7][:, P:P + ES]).then_inc(setup_done, 1)
                for g in range(PER):
                    act.sem_inc(g_free[g], 1)
                for k in range(2):
                    act.sem_inc(z_free[k], 1)

                def gathered(n, k):
                    place = G[:, :, bass.ds(n * 4 * PER, 4 * PER)].rearrange("p e (t g) -> p t g e", g=PER)
                    for g in range(PER):
                        act.wait_ge(g_full[g], 1).then_inc(g_full[g], -1)
                        if g == PER - 1:
                            act.sem_inc(z_free[k], 1)
                        nc.scalar.copy(place[:, :, g, :], ps[3 + g][:, :].rearrange("p (t e) -> p t e", t=4)).then_inc(g_free[g], 1)

                def select(k, before):
                    act.wait_ge(zT_full, 1).then_inc(zT_full, -1)
                    nc.scalar.copy(zT[:, :], ps[0][:, :]).then_inc(zT_ready, 1)
                    if before is not None:
                        gathered(before, 1 - k)
                    act.wait_ge(perm_full, 1).then_inc(perm_full, -1)
                    nc.scalar.copy(taken[k][:, :, :], ps[2][:, :].rearrange("p (t e) -> p t e", t=4)).then_inc(taken_ready[k], 1)

                LAST = TILES // 4 - 1
                select(0, None)
                with act.Fori(0, TILES // 8 - 1) as i:
                    for k in range(2):
                        select(1 - k, 2 * i + k)
                select(1, LAST - 1)
                gathered(LAST, 1)

            @block.vector
            def _(dve):
                dve.wait_ge(iota_done, 1)
                nc.vector.tensor_scalar(tie[:, :], tie_i[:, :], 1e-6 / (GROUP - 1), None, ALU.mult).then_inc(step, 1)
                dve.wait_ge(step, 1).then_inc(step, -1)
                with dve.Fori(0, TILES // 8) as i:
                    tile_stats(nc, dve, step, x, i * 8, bn, mv, mean, var)
                newton_rsqrt(nc.vector, dve, step, rstd[:, :], var[:, :], tmp[:, :])
                dve.sem_inc(rstd_ready, 1)
                dve.wait_ge(loaded, 64)
                with dve.Fori(0, TILES // 8) as i:
                    for k in range(2):
                        dve.wait_ge(z_ready[k], 1).then_inc(z_ready[k], -1)
                        nc.vector.tensor_copy(zh[k][:, :, :], z[k][:, :, :]).then_inc(step, 1)
                        dve.wait_ge(step, 1).then_inc(step, -1)
                        nc.vector.tensor_tensor(zl[k][:, :, :], z[k][:, :, :], zh[k][:, :, :].bitcast(F32), ALU.subtract).then_inc(z_split, 1)
                        dve.wait_ge(logits, 1).then_inc(logits, -1)
                        nc.vector.scalar_tensor_tensor(L[:, :], ps[1][:, :], bcol[:, 0:1], tie[:, :], ALU.add, ALU.add).then_inc(step, 1)
                        dve.wait_ge(step, 1).then_inc(step, -1)
                        nc.vector.tensor_reduce(top[:, :], L[:, :].rearrange("p (n t) -> p n t", t=GROUP), AX.X, ALU.max).then_inc(step, 1)
                        dve.wait_ge(step, 1).then_inc(step, -1)
                        nc.vector.tensor_tensor(pT4[:, :, :].rearrange("p a (n t) -> p (a n) t", t=GROUP), L[:, :].rearrange("p (n t) -> p n t", t=GROUP), top[:, :].unsqueeze(2).to_broadcast([P, 16, GROUP]), ALU.is_equal).then_inc(step, 1)
                        dve.wait_ge(step, 1).then_inc(step, -1)
                        dve.sem_inc(perm_ready, 1)
                        nc.vector.tensor_copy(permT[:, bass.ds(8 * i + 4 * k, 4), :], pT4[:, :, :]).then_inc(step, 1)
                        dve.wait_ge(step, 1).then_inc(step, -1)

        with ExitStack() as experts:
            sb2 = lambda n, s, d=F32: experts.enter_context(nc.sbuf_tensor(pre + n, s, d))
            w1 = [sb2(f"w1_{j}", [P, 4, NS, F]) for j in range(2)]
            w2 = [sb2(f"w2_{j}", [P, 4, NS, F]) for j in range(2)]
            w2T = [sb2(f"w2T{j}", [P, 4, P]) for j in range(2)]
            b1e = [sb2(f"b1e{j}", [P, 4]) for j in range(2)]
            g_now = [sb2(f"g_now{k}", [P, NS, NG]) for k in range(2)]
            h = [sb2(f"h{k}", [P, NG]) for k in range(4)]
            w_loaded = [sem(f"w_loaded{j}") for j in range(2)]
            w_free = [sem(f"w_free{j}") for j in range(2)]
            w2_full = sem("w2_full")
            w2T_ready = sem("w2T_ready")
            b1e_ready = sem("b1e_ready")
            g_copied = sem("g_copied")
            g_now_free = sem("g_now_free")
            h_full = sem("h_full")
            h_ready = sem("h_ready")
            r_full = [sem(f"r_full{s}") for s in range(NS)]
            r_free = [sem(f"r_free{s}") for s in range(NS)]
            block = experts.enter_context(nc.Block(pre + "experts"))

            @block.sync
            def _(sp):
                with sp.Fori(0, NE // 8) as i:
                    for j in range(2):
                        sp.wait_ge(w_free[j], 1).then_inc(w_free[j], -1)
                        for dst, src in ((w1[j], W1), (w2[j], W2)):
                            for k in range(4):
                                sp.dma_start(dst[:, k, :, :], src[bass.ds(8 * i + 4 * j + k, 1)].rearrange("a s d f -> d (a s) f")).then_inc(w_loaded[j], 16)

            @block.tensor
            def _(pe):
                def result(k):
                    for s in range(NS):
                        rows = slice(F * s, F * s + F)
                        if k % 4 == 0:
                            pe.wait_ge(r_free[s], 1).then_inc(r_free[s], -1)
                        ins = nc.tensor.matmul(ps[4 + s][:, P * (k % 4):P * (k % 4) + P], w2T[k // 4][rows, k % 4, :], h[k % 4][rows, :], start=True, stop=True)
                        if k % 4 == 3:
                            ins.then_inc(r_full[s], 1)

                with pe.Fori(0, NE // 8) as i:
                    for k in range(8):
                        j = k // 4
                        if k % 4 == 0:
                            pe.wait_ge(w_loaded[j], 8 * 16).then_inc(w_loaded[j], -8 * 16)
                            for n in range(4):
                                ins = nc.tensor.transpose(ps[j][:, P * n:P * n + P], w2[j][:, n, :, :], ident[:, :])
                            ins.then_inc(w2_full, 1)
                        pe.wait_ge(g_copied, 1).then_inc(g_copied, -1)
                        if k > 1:
                            pe.wait_ge(h_ready, 1).then_inc(h_ready, -1)
                        for s in range(NS):
                            ins = nc.tensor.matmul(ps[2 + k % 2][F * s:F * s + F, 0:NG], w1[j][:, k % 4, s, :], g_now[k % 2][:, s, :], start=True, stop=True)
                        ins.then_inc(h_full, 1)
                        if k % 4 == 2:
                            pe.wait_ge(w2T_ready, 1).then_inc(w2T_ready, -1)
                        if k > 1:
                            result(k - 2)
                    for k in (6, 7):
                        pe.wait_ge(h_ready, 1).then_inc(h_ready, -1)
                        result(k)

            @block.scalar
            def _(act):
                for j in range(2):
                    act.sem_inc(w_free[j], 1)
                    act.sem_inc(g_now_free, 1)
                for s in range(NS):
                    act.sem_inc(r_free[s], 1)
                with act.Fori(0, NE // 8) as i:
                    for k in range(8):
                        j = k // 4
                        if k % 4 == 0:
                            act.wait_ge(w2_full, 1).then_inc(w2_full, -1)
                            nc.scalar.copy(w2T[j][:, :, :], ps[j][:, :].rearrange("p (n d) -> p n d", n=4)).then_inc(w2T_ready, 1)
                            nc.scalar.copy(b1e[j][:, :], b1T[:, bass.ds(8 * i + 4 * j, 4)]).then_inc(b1e_ready, 1)
                            act.wait_ge(b1e_ready, 1).then_inc(b1e_ready, -1)
                        act.wait_ge(h_full, 1).then_inc(h_full, -1)
                        act.sem_inc(g_now_free, 1)
                        if k % 4 == 3:
                            act.sem_inc(w_free[j], 1)
                        nc.scalar.activation(h[k % 4][:, :], ps[2 + k % 2][:, 0:NG], ACT.Relu, bias=b1e[j][:, k % 4:k % 4 + 1]).then_inc(h_ready, 1)

            @block.vector
            def _(dve):
                def add_bias(i, j):
                    bias = b2T[:, bass.ds((8 * i + 4 * j) * NS, 4 * NS)].rearrange("p (k s) -> p k s", s=NS)
                    place = R[:, :, bass.ds((8 * i + 4 * j) * NS, 4 * NS)].rearrange("p n (k s) -> p s k n", s=NS)
                    for s in range(NS):
                        dve.wait_ge(r_full[s], 1).then_inc(r_full[s], -1)
                        nc.vector.tensor_tensor(place[:, s, :, :], ps[4 + s][:, :].rearrange("p (k n) -> p k n", k=4), bias[:, :, s].unsqueeze(2).to_broadcast([P, 4, NG]), ALU.add).then_inc(r_free[s], 1)

                with dve.Fori(0, NE // 8) as i:
                    for k in range(8):
                        dve.wait_ge(g_now_free, 1).then_inc(g_now_free, -1)
                        nc.vector.tensor_copy(g_now[k % 2][:, :, :], G[:, bass.ds((8 * i + k) * NS, NS), :]).then_inc(g_copied, 1)
                        if k == 5:
                            add_bias(i, 0)
                    add_bias(i, 1)

        with ExitStack() as back:
            sb3 = lambda n, s, d=F32: back.enter_context(nc.sbuf_tensor(pre + n, s, d))
            Rs = [sb3(f"Rs{k}", [P, PER, ES]) for k in range(2)]
            Rt = [sb3(f"Rt{k}", [P, PER, P]) for k in range(2)]
            pT = [sb3(f"pT{k}", [P, 4, P]) for k in range(2)]
            rs_ready = sem("rs_ready")
            rs_free = sem("rs_free")
            pT_ready = sem("pT_ready")
            pT_free = sem("pT_free")
            rt_full = sem("rt_full")
            rt_ready = sem("rt_ready")
            y_full = sem("y_full")
            y_free = sem("y_free")
            block = back.enter_context(nc.Block(pre + "back"))

            @block.gpsimd
            def _(pool):
                with pool.Fori(0, TILES // 8) as i:
                    for k in range(2):
                        pool.wait_ge(pT_free, 1).then_inc(pT_free, -1)
                        nc.gpsimd.tensor_copy(pT[k][:, :, :], permT[:, bass.ds(8 * i + 4 * k, 4), :]).then_inc(pT_ready, 1)

            @block.tensor
            def _(pe):
                def give(k, t):
                    if t == 0:
                        pe.wait_ge(pT_ready, 1).then_inc(pT_ready, -1)
                        pe.wait_ge(y_free, 1).then_inc(y_free, -1)
                    pe.wait_ge(rt_ready, 1).then_inc(rt_ready, -1)
                    for g in range(PER):
                        rows = slice(GROUP * g, GROUP * g + GROUP)
                        ins = nc.tensor.matmul(ps[4 + k][rows, P * t:P * t + P], pT[k][:, t, rows], Rt[t % 2][:, g, :], start=True, stop=True)
                    if t == 3:
                        ins.then_inc(y_full, 1)

                with pe.Fori(0, TILES // 8) as i:
                    for n in range(8):
                        k, t = n // 4, n % 4
                        pe.wait_ge(rs_ready, 1).then_inc(rs_ready, -1)
                        for g in range(PER):
                            ins = nc.tensor.transpose(ps[2 + t % 2][:, P * g:P * g + P], Rs[t % 2][:, g, :], ident[:, :])
                        ins.then_inc(rt_full, 1)
                        if n > 0:
                            give((n - 1) // 4, (n - 1) % 4)
                    give(1, 3)

            @block.scalar
            def _(act):
                for k in range(2):
                    act.sem_inc(rs_free, 1)
                    act.sem_inc(pT_free, 1)
                    act.sem_inc(y_free, 1)
                with act.Fori(0, TILES // 8) as i:
                    for n in range(8):
                        act.wait_ge(rt_full, 1).then_inc(rt_full, -1)
                        act.sem_inc(rs_free, 1)
                        nc.scalar.copy(Rt[n % 2][:, :, :], ps[2 + n % 2][:, :].rearrange("p (g d) -> p g d", g=PER)).then_inc(rt_ready, 1)

            @block.vector
            def _(dve):
                def add(i, k):
                    dve.wait_ge(y_full, 1).then_inc(y_full, -1)
                    dve.sem_inc(pT_free, 1)
                    tiles = x[:, bass.ds(8 * i + 4 * k, 4), :]
                    nc.vector.scalar_tensor_tensor(tiles, ps[4 + k][:, :].rearrange("p (t d) -> p t d", t=4), 0.5, tiles, ALU.mult, ALU.add).then_inc(y_free, 1)

                with dve.Fori(0, TILES // 8) as i:
                    for n in range(8):
                        dve.wait_ge(rs_free, 1).then_inc(rs_free, -1)
                        nc.vector.tensor_copy(Rs[n % 2][:, :, :], R[:, bass.ds((8 * i + n) * PER, PER), :]).then_inc(rs_ready, 1)
                        if n == 6:
                            add(i, 0)
                    add(i, 1)

        nc.all_engine_barrier()
        nc.clear_and_free_semaphores(signals)
        nc.all_engine_barrier()


def prepare_attention(nc, x, ident, dram, outs, slopes):
    gamma, w_q, w_kv, null_kv, q_scale, k_scale, w_out = dram
    xnT, wo, scales, dist, null_dist, slope, null_keys, nvo = outs
    TILES = x.shape[1]
    HP = wo.shape[1] - 1
    HEADS, _, DH = null_kv.shape
    ROWS = HEADS * 4
    NT = null_dist.shape[1]
    NB = TILES // NT
    FAR = dist.shape[1] - P
    with ExitStack() as ctx:
        sb = lambda n, s, d=F32: ctx.enter_context(nc.sbuf_tensor("p_" + n, s, d))
        sem = lambda n: ctx.enter_context(nc.semaphore("p_" + n))
        ps = [ctx.enter_context(nc.psum_tensor(f"p_ps{k}", [P, 4 * P], F32)) for k in range(5)]
        bn = sb("bn", [P, 8, 6])
        mv = sb("mv", [P, 8, 2])
        mean = sb("mean", [P, TILES])
        var = sb("var", [P, TILES])
        rstd = sb("rstd", [P, TILES])
        rstd2 = sb("rstd2", [P, TILES])
        tmp = sb("tmp", [P, TILES])
        zn = sb("zn", [P, 2, 4, P])
        gcol = sb("gcol", [P, 1])
        qs = sb("qs", [P, DH])
        ks = sb("ks", [P, DH])
        qs_col = sb("qs_col", [P, 1])
        ks_col = sb("ks_col", [P, 1])
        row_scales = sb("row_scales", [P, DH])
        identr = sb("identr", [P, P], F32R)
        nk = sb("nk", [ROWS, 2, DH])
        nsq = sb("nsq", [ROWS, DH])
        ns = sb("ns", [ROWS, 1])
        nr = sb("nr", [ROWS, 1])
        nt = sb("nt", [ROWS, 1])
        nkn = sb("nkn", [ROWS, 2, DH])
        nhi = sb("nhi", [ROWS, 2, DH], F32R)
        nlo = sb("nlo", [ROWS, 2, DH], F32R)
        nvb = sb("nvb", [P, HP, 4, 4 * HP])
        blk = sb("blk", [P, 4, P])
        dist_i = sb("dist_i", [P, FAR + P], I32)
        null_dist_i = sb("null_dist_i", [P, NT, 2], I32)

        loaded = sem("loaded")
        pool_step = sem("pool_step")
        iotas = sem("iotas")
        dist_float = sem("dist_float")
        masks = sem("masks")
        step = sem("step")
        null_split = sem("null_split")
        null_full = sem("null_full")
        nvb_ready = sem("nvb_ready")
        nvo_full = sem("nvo_full")
        zn_ready = [sem(f"zn_ready{k}") for k in range(2)]
        zT_full = [sem(f"zT_full{k}") for k in range(2)]
        zn_free = [sem(f"zn_free{k}") for k in range(2)]

        block = ctx.enter_context(nc.Block("prepare"))

        @block.sync
        def _(sp):
            sp.dma_start(gcol[:, :], gamma.unsqueeze(1)).then_inc(loaded, 16)
            sp.dma_start(qs[:, :], q_scale.unsqueeze(0).to_broadcast([P, DH])).then_inc(loaded, 16)
            sp.dma_start(ks[:, :], k_scale.unsqueeze(0).to_broadcast([P, DH])).then_inc(loaded, 16)
            for k in range(2):
                sp.dma_start(nk[:, k, :], null_kv.rearrange("h c d -> (h c) d")).then_inc(loaded, 16)
            for k in range(2):
                sp.dma_start(qs_col[DH * k:DH * k + DH, :], q_scale.unsqueeze(1)).then_inc(loaded, 16)
                sp.dma_start(ks_col[DH * k:DH * k + DH, :], k_scale.unsqueeze(1)).then_inc(loaded, 16)
            sp.dma_start(wo[:, 1:HP + 1, :], w_out.rearrange("(m p) n -> p m n", p=P)).then_inc(loaded, 16)
            sp.wait_ge(loaded, 10 * 16)

        @block.gpsimd
        def _(pool):
            nc.gpsimd.iota(dist_i[:, :], [[1, FAR + P]], base=-FAR, channel_multiplier=-1)
            nc.gpsimd.iota(null_dist_i[:, :, :], [[P, NT], [-1, 2]], base=2, channel_multiplier=1).then_inc(iotas, 1)
            nc.gpsimd.memset(blk[:, :, :], 1.0)
            nc.gpsimd.memset(nvb[:, :, :, :], 0.0)
            nc.gpsimd.memset(wo[:, 0:1, :], 0.0)
            for h, m in enumerate(slopes + slopes[0:2]):
                ins = nc.gpsimd.memset(slope[:, h:h + 1], float(m))
            ins.then_inc(pool_step, 1)
            pool.wait_ge(pool_step, 1).then_inc(pool_step, -1)
            nc.gpsimd.affine_select(out=blk[:, :, :], in_=blk[:, :, :], compare_op=ALU.is_ge, fill=0.0, base=0, pattern=[[-32, 4], [0, P]], channel_multiplier=1).then_inc(pool_step, 1)
            pool.wait_ge(pool_step, 1).then_inc(pool_step, -1)
            nc.gpsimd.affine_select(out=blk[:, :, :], in_=blk[:, :, :], compare_op=ALU.is_ge, fill=0.0, base=31, pattern=[[32, 4], [0, P]], channel_multiplier=-1).then_inc(masks, 1)
            pool.wait_ge(dist_float, 1).then_inc(dist_float, -1)
            nc.gpsimd.affine_select(out=dist[:, :], in_=dist[:, :], compare_op=ALU.is_ge, fill=-1e37, base=FAR, pattern=[[-1, FAR + P]], channel_multiplier=1).then_inc(pool_step, 1)
            pool.wait_ge(pool_step, 1)

        @block.tensor
        def _(pe):
            with pe.Fori(0, TILES // 8) as i:
                for k in range(2):
                    pe.wait_ge(zn_ready[k], 1).then_inc(zn_ready[k], -1)
                    for t in range(4):
                        ins = nc.tensor.transpose(ps[k][:, P * t:P * t + P], zn[:, k, t, :], ident[:, :])
                    ins.then_inc(zT_full[k], 1)
            pe.wait_ge(null_split, 1).then_inc(null_split, -1)
            nc.tensor.transpose(ps[2][:, 0:ROWS].bitcast(F32R), nhi[:, :, :], identr[0:ROWS, 0:ROWS])
            nc.tensor.transpose(ps[2][:, P:P + ROWS].bitcast(F32R), nlo[:, :, :], identr[0:ROWS, 0:ROWS])
            nc.tensor.transpose(ps[2][:, 2 * P:2 * P + ROWS], nk[:, :, :], ident[0:ROWS, 0:ROWS]).then_inc(null_full, 1)
            pe.wait_ge(nvb_ready, 1).then_inc(nvb_ready, -1)
            for m in range(HP):
                ins = nc.tensor.matmul(ps[3][:, 0:P], nvb[:, m, :, :], wo[:, m + 1, :], start=(m == 0), stop=(m == HP - 1))
            ins.then_inc(nvo_full, 1)

        @block.scalar
        def _(act):
            act.wait_ge(loaded, 10 * 16)
            for k in range(2):
                act.sem_inc(zn_free[k], 1)
            flat = xnT[:, :, :].rearrange("p b n -> p (b n)")
            with act.Fori(0, TILES // 8) as i:
                for k in range(2):
                    act.wait_ge(zT_full[k], 1).then_inc(zT_full[k], -1)
                    nc.scalar.activation(flat[:, bass.ds((2 * i + k) * 4 * P, 4 * P)], ps[k][:, :], ACT.Copy, scale=gcol[:, 0:1]).then_inc(zn_free[k], 1)

        @block.vector
        def _(dve):
            nc.vector.tensor_copy(identr[:, :], ident[:, :]).then_inc(step, 1)
            dve.wait_ge(step, 1).then_inc(step, -1)
            dve.wait_ge(iotas, 1)
            nc.vector.tensor_copy(dist[:, :], dist_i[:, :]).then_inc(step, 1)
            dve.wait_ge(step, 1).then_inc(step, -1)
            nc.vector.tensor_copy(null_dist[:, :, :], null_dist_i[:, :, :]).then_inc(dist_float, 1)
            with dve.Fori(0, TILES // 8) as i:
                tile_stats(nc, dve, step, x, i * 8, bn, mv, mean, var)
            newton_rsqrt(nc.vector, dve, step, rstd[:, :], var[:, :], tmp[:, :])
            nc.vector.tensor_scalar(var[:, :], var[:, :], EPS, None, ALU.subtract).then_inc(step, 1)
            dve.wait_ge(step, 1).then_inc(step, -1)
            for _ in range(2):
                nc.vector.tensor_tensor(var[:, :], var[:, :], rstd[:, :], ALU.mult).then_inc(step, 1)
                dve.wait_ge(step, 1).then_inc(step, -1)
            nc.vector.tensor_scalar(var[:, :], var[:, :], EPS, None, ALU.add).then_inc(step, 1)
            dve.wait_ge(step, 1).then_inc(step, -1)
            newton_rsqrt(nc.vector, dve, step, rstd2[:, :], var[:, :], tmp[:, :])
            nc.vector.tensor_tensor(rstd[:, :], rstd[:, :], rstd2[:, :], ALU.mult).then_inc(step, 1)
            dve.wait_ge(step, 1).then_inc(step, -1)
            with dve.Fori(0, TILES // 8) as i:
                for k in range(2):
                    four = bass.ds(8 * i + 4 * k, 4)
                    dve.wait_ge(zn_free[k], 1).then_inc(zn_free[k], -1)
                    nc.vector.tensor_tensor(zn[:, k, :, :], x[:, four, :], mean[:, four].unsqueeze(2).to_broadcast([P, 4, P]), ALU.subtract).then_inc(step, 1)
                    dve.wait_ge(step, 1).then_inc(step, -1)
                    nc.vector.tensor_tensor(zn[:, k, :, :], zn[:, k, :, :], rstd[:, four].unsqueeze(2).to_broadcast([P, 4, P]), ALU.mult).then_inc(zn_ready[k], 1)
            dve.wait_ge(loaded, 10 * 16)
            nc.vector.scalar_tensor_tensor(scales[:, :], qs_col[:, :], 8.0, ks_col[:, :], ALU.mult, ALU.mult)
            nc.vector.scalar_tensor_tensor(row_scales[:, :], qs[:, :], 8.0, ks[:, :], ALU.mult, ALU.mult).then_inc(step, 1)
            dve.wait_ge(step, 1).then_inc(step, -1)
            nc.vector.tensor_tensor(nsq[:, :], nk[:, 0, :], nk[:, 0, :], ALU.mult).then_inc(step, 1)
            dve.wait_ge(step, 1).then_inc(step, -1)
            nc.vector.tensor_reduce(ns[:, :], nsq[:, :], AX.X, ALU.add).then_inc(step, 1)
            dve.wait_ge(step, 1).then_inc(step, -1)
            nc.vector.tensor_scalar(ns[:, :], ns[:, :], 1e-24, None, ALU.max).then_inc(step, 1)
            dve.wait_ge(step, 1).then_inc(step, -1)
            newton_rsqrt(nc.vector, dve, step, nr[:, :], ns[:, :], nt[:, :])
            nc.vector.scalar_tensor_tensor(nkn[:, :, :], nk[:, :, :], nr[:, 0:1], row_scales[0:ROWS, :].unsqueeze(1).to_broadcast([ROWS, 2, DH]), ALU.mult, ALU.mult).then_inc(step, 1)
            dve.wait_ge(step, 1).then_inc(step, -1)
            nc.vector.tensor_copy(nhi[:, :, :], nkn[:, :, :]).then_inc(step, 1)
            dve.wait_ge(step, 1).then_inc(step, -1)
            nc.vector.tensor_tensor(nlo[:, :, :], nkn[:, :, :], nhi[:, :, :].bitcast(F32), ALU.subtract).then_inc(null_split, 1)
            dve.wait_ge(null_full, 1).then_inc(null_full, -1)
            for part in range(2):
                keys = ps[2][:, P * part:P * part + ROWS].rearrange("p (h c) -> p h c", c=4)[:, :, 0:4:2]
                pairs = keys.rearrange("p (m h) c -> p m h c", h=2)
                nc.vector.tensor_copy(null_keys[:, 0:HP, part, :, :], pairs)
                nc.vector.tensor_copy(null_keys[:, HP:HP + 1, part, :, :], pairs[:, 0:1])
            dve.wait_ge(masks, 1)
            values = ps[2][:, 2 * P:2 * P + ROWS].rearrange("p (h c) -> p h c", c=4)[:, :, 1:4:2]
            for m in range(HP):
                for h in range(2):
                    ins = nc.vector.tensor_copy(nvb[DH * h:DH * h + DH, m, :, 4 * m + 2 * h:4 * m + 2 * h + 2], values[DH * h:DH * h + DH, 2 * m + h, :].unsqueeze(1).to_broadcast([DH, 4, 2]))
            ins.then_inc(nvb_ready, 1)
            dve.wait_ge(nvo_full, 1).then_inc(nvo_full, -1)
            nc.vector.tensor_tensor(nvo[:, :, :], blk[:, :, :], ps[3][:, 0:P].unsqueeze(1).to_broadcast([P, 4, P]), ALU.mult).then_inc(step, 1)
            dve.wait_ge(step, 1).then_inc(step, -1)


def attention(nc, x, ident, dram):
    gamma, w_q, w_kv, null_kv, q_scale, k_scale, w_out = dram
    HEADS, NULL, DH = null_kv.shape[0], null_kv.shape[1] // 2, null_kv.shape[2]
    NB = 4
    HP = HEADS // 2
    NT = x.shape[1] // NB
    N = NT * P
    FAR = N
    QK = 2 * P
    start = 2.0 ** (-2.0 ** (-(4 - 3.0)))
    slopes = [start * start ** i for i in range(HEADS)]
    RING = 3
    with ExitStack() as ctx:
        sb = lambda n, s, d=F32: ctx.enter_context(nc.sbuf_tensor("a_" + n, s, d))
        sem = lambda n: ctx.enter_context(nc.semaphore("a_" + n))

        xnT = sb("xnT", [P, NB, N])
        wo = sb("wo", [P, HP + 1, P])
        scales = sb("scales", [P, 1])
        dist = sb("dist", [P, FAR + P])
        null_dist = sb("null_dist", [P, NT, NULL])
        slope = sb("slope", [P, HEADS + 2])
        null_keys = sb("null_keys", [P, HP + 1, 2, 2, NULL], F32R)
        nvo = sb("nvo", [P, 4, P])

        prepare_attention(nc, x, ident, dram, (xnT, wo, scales, dist, null_dist, slope, null_keys, nvo), slopes)

        qT = [sb(f"qT{r}", [P, 2, N], F32R) for r in range(2)]
        khT = [sb(f"khT{r}", [P, 2, N], F32R) for r in range(2)]
        klT = [sb(f"klT{r}", [P, 2, N], F32R) for r in range(2)]
        qkv = [sb(f"qkv{r}", [P, NT, 3 * P]) for r in range(2)]
        null_neg = [sb(f"null_neg{r}", [P, NT, 2, NULL]) for r in range(2)]
        null_min = [sb(f"null_min{r}", [P, NT, 2]) for r in range(2)]
        w_now = sb("w_now", [P, 3 * P])
        null_now = sb("null_now", [P, 2, 2, NULL], F32R)
        slope_now = sb("slope_now", [P, 2])
        table = sb("table", [P, 2, FAR + P])
        square = sb("square", [P, NT // 2, 4, DH])
        norm2 = sb("norm2", [P, NT // 2, 4])
        rnorm = sb("rnorm", [P, NT // 2, 4])
        unit = [sb(f"unit{g}", [P, NT // 2, 4, 2, DH]) for g in range(2)]
        ntmp = sb("ntmp", [P, NT // 2, 4])
        prob = [sb(f"prob{k}", [P, 2, N]) for k in range(2)]
        probT = [sb(f"probT{k}", [P, 2, N]) for k in range(2)]
        neg_max = sb("neg_max", [P, NT, 2])
        row_sum = sb("row_sum", [P, NT, 2])
        null_arg = sb("null_arg", [P, NT // 2, 2, NULL])
        null_prob = sb("null_prob", [P, NT // 2, 2, NULL])
        total = sb("total", [P, NT // 2, 2])
        rtotal = sb("rtotal", [P, NT // 2, 2])
        rtotal_wide = sb("rtotal_wide", [P, NT // 2, 2, DH])
        null_all = sb("null_all", [P, NB, NT, 4 * HP])
        oT = sb("oT", [P, 4 * P])
        nullT = oT[:, 0:P]

        score = [ctx.enter_context(nc.psum_tensor(f"a_score{h}", [P, N], F32)) for h in range(2)]
        ring = [ctx.enter_context(nc.psum_tensor(f"a_ring{k}", [P, 4 * P], F32)) for k in range(RING)]
        outT = ctx.enter_context(nc.psum_tensor("a_outT", [P, 4 * P], F32))

        step = sem("step")
        pool_step = sem("pool_step")
        zeroed = sem("zeroed")
        score_full = [sem(f"score_full{h}") for h in range(2)]
        score_free = [sem(f"score_free{h}") for h in range(2)]
        shifted = [sem(f"shifted{h}") for h in range(2)]
        prob_ready = [sem(f"prob_ready{h}") for h in range(2)]
        to_act = [sem(f"to_act{k}") for k in range(RING)]
        to_dve = [sem(f"to_dve{k}") for k in range(RING)]
        freed = [sem(f"freed{k}") for k in range(RING)]
        high_ready = sem("high_ready")
        o_full = sem("o_full")
        o_copied = sem("o_copied")
        null_arg_ready = sem("null_arg_ready")
        null_prob_ready = sem("null_prob_ready")
        rtotal_ready = sem("rtotal_ready")
        projected = sem("projected")
        squared = sem("squared")
        summed = sem("summed")
        normed = sem("normed")
        unit_free = sem("unit_free")
        w_free = sem("w_free")
        w_loaded = sem("w_loaded")
        null_loaded = sem("null_loaded")
        nullT_ready = sem("nullT_ready")

        fill = {
            0: ([("PV", 7), ("O", 1)], [("PROJ", 0), ("PROJ", 1)], [("PROJ", 2)], [("PROJ", 3), ("RB", 1)]),
            1: ([("SQ", 0)], [], [], [("Y", 1), ("PROJ", 4), ("PROJ", 5)]),
            2: ([("RS", 0), ("PV", 0)], [], [("PV", 1), ("NM", 0), ("PROJ", 6)], []),
            3: ([], [], [("PV", 2), ("PROJ", 7)], []),
            4: ([], [("R2", 0)], [("PV", 3), ("O", 0)], [("RB", 0)]),
            5: ([("SLOPE",)], [], [("SQ", 1), ("RS", 1), ("C", 0, 0), ("C", 0, 1), ("C", 0, 2)], []),
            6: ([("Y", 0), ("PV", 4)], [], [("C", 0, 3), ("PV", 5)], [("NULL", 0), ("NM", 1), ("C", 1, 0), ("C", 1, 1), ("PV", 6)]),
            7: ([], [], [], [("NULL", 1), ("C", 1, 2), ("C", 1, 3), ("R2", 1)]),
        }
        plan = []
        for t in range(NT):
            u = (t + 1) % NT
            plan += [("S", u, 0)] + fill[t][0] + [("T", t, 0), ("S", u, 1)] + fill[t][1]
            plan += [("TAB", 0)] * (u == 0) + [("SM", u, 0), ("T", t, 1)] + [("R1", t // 4)] * (t % 4 == 3) + fill[t][2]
            plan += [("TAB", 1)] * (u == 0) + [("SM", u, 1)] + fill[t][3]
        bank, fills = {}, 0
        for s in plan:
            for g in range(1 + (s[0] == "T" and s[1] >= 4)):
                if s[0] in ("T", "C", "PROJ", "NULL", "RB", "Y"):
                    bank[s, g] = fills % RING
                    fills += 1
        first = [s for s in plan if s[0] in ("PROJ", "SQ", "RS", "NM", "C", "NULL", "SLOPE", "TAB") or s[0] in ("S", "SM") and s[1] == 0]
        rest = [("PV", 7), ("O", 1), ("RB", 1), ("Y", 1)]

        def turns(eng, run):
            run(first, -1, NB - 1)
            with eng.Fori(0, HP) as hp:
                for b in range(NB):
                    run(plan, hp, b)
            run(rest, HP, 0)

        block = ctx.enter_context(nc.Block("attention"))

        @block.sync
        def _(sp):
            def load(pair):
                for part, w in enumerate((w_q, w_kv[:, 0:HP * P], w_kv[:, HP * P:2 * HP * P])):
                    sp.dma_start(w_now[:, P * part:P * part + P].unsqueeze(1), w.rearrange("p (m n) -> p m n", n=P)[:, bass.ds(pair, 1), :]).then_inc(w_loaded, 16)

            load(0)
            with sp.Fori(1, HP) as pair:
                sp.wait_ge(w_free, 1).then_inc(w_free, -1)
                load(pair)
            sp.wait_ge(w_free, 1).then_inc(w_free, -1)
            load(0)

        @block.gpsimd
        def _(pool):
            def run(steps, hp, b):
                for s in steps:
                    if s[0] in ("SQ", "NM"):
                        four = slice(4 * s[1], 4 * s[1] + 4)
                        qk = qkv[(b + 1) % 2][:, four, 0:QK]
                    if s[0] == "SQ":
                        pool.wait_ge(projected, 1).then_inc(projected, -1)
                        nc.gpsimd.tensor_tensor(square[:, :, :, :].rearrange("p t v d -> p t (v d)"), qk, qk, ALU.mult).then_inc(squared, 1)
                    if s[0] == "NM":
                        pool.wait_ge(summed, 1).then_inc(summed, -1)
                        newton_rsqrt(nc.gpsimd, pool, pool_step, rnorm[:, :, :], norm2[:, :, :], ntmp[:, :, :])
                        vectors = qk.rearrange("p t (v d) -> p t v d", d=DH)
                        pool.wait_ge(unit_free, 1).then_inc(unit_free, -1)
                        for c in range(2):
                            ins = nc.gpsimd.tensor_tensor(unit[s[1]][:, :, :, c, :], vectors, rnorm[:, :, :].unsqueeze(3).to_broadcast([P, 4, 4, DH]), ALU.mult)
                        ins.then_inc(normed, 1)

            nc.gpsimd.memset(qkv[1][:, :, :], 0.0)
            nc.gpsimd.memset(probT[1][:, :, :], 0.0)
            nc.gpsimd.memset(rtotal_wide[:, :, :, :], 0.0).then_inc(zeroed, 1)
            turns(pool, run)

        @block.tensor
        def _(pe):
            def run(steps, hp, b):
                r, n = b % 2, (b + 1) % 2
                for s in steps:
                    if steps is first and s[0] in ("S", "NULL"):
                        for k in range(RING):
                            pe.wait_ge(freed[k], 1)
                    if s[0] == "S":
                        _, t, h = s
                        q = r if t else n
                        pe.wait_ge(score_free[h], 1).then_inc(score_free[h], -1)
                        for c in range(0, P * (t + 1), 4 * P):
                            e = min(c + 4 * P, P * (t + 1))
                            nc.tensor.matmul(score[h][:, c:e], qT[q][:, h, P * t:P * t + P], khT[q][:, h, c:e], start=True, stop=False)
                            ins = nc.tensor.matmul(score[h][:, c:e], qT[q][:, h, P * t:P * t + P], klT[q][:, h, c:e], start=False, stop=True)
                        ins.then_inc(score_full[h], 1)
                    if s[0] == "T":
                        _, t, h = s
                        pe.wait_ge(prob_ready[h], 1).then_inc(prob_ready[h], -1)
                        for g in range(1 + (t >= 4)):
                            k = bank[s, g]
                            pe.wait_ge(freed[k], 1).then_inc(freed[k], -1)
                            for j in range(4 * g, min(4 * g + 4, t + 1)):
                                ins = nc.tensor.transpose(ring[k][:, P * (j % 4):P * (j % 4) + P], prob[t % 2][:, h, P * j:P * j + P], ident[:, :])
                            ins.then_inc((to_act, to_dve)[h][k], 1)
                    if s[0] == "PV":
                        t = s[1]
                        v = qkv[n if t == 7 else r]
                        if steps is rest:
                            for k in range(RING):
                                pe.wait_ge(freed[k], 1)
                        for j in range(t + 1):
                            for h in range(2):
                                ins = nc.tensor.matmul(outT[DH * h:DH * h + DH, P * (t % 4):P * (t % 4) + P], v[:, j, QK + DH * h:QK + DH * h + DH], probT[t % 2][:, h, P * j:P * j + P], start=(j == 0), stop=(j == t))
                        if t % 4 == 3:
                            ins.then_inc(o_full, 1)
                    if s[0] == "RB":
                        k = bank[s, 0]
                        pe.wait_ge(rtotal_ready, 1).then_inc(rtotal_ready, -1)
                        pe.wait_ge(freed[k], 1).then_inc(freed[k], -1)
                        for t in range(4):
                            ins = nc.tensor.transpose(ring[k][:, P * t:P * t + P], rtotal_wide[:, t, :, :], ident[:, :])
                        ins.then_inc(to_dve[k], 1)
                    if s[0] == "Y":
                        k = bank[s, 0]
                        if steps is rest:
                            pe.wait_ge(freed[bank[("RB", 1), 0]], 1)
                        pe.wait_ge(freed[k], 1).then_inc(freed[k], -1)
                        pair = hp + 1 if s[1] == 0 or b > 0 else hp
                        for t in range(4):
                            ins = nc.tensor.matmul(ring[k][:, P * t:P * t + P], oT[:, P * t:P * t + P], wo[:, bass.ds(pair, 1), :], start=True, stop=True)
                        ins.then_inc(to_dve[k], 1)
                    if s[0] == "PROJ":
                        t = s[1]
                        k = bank[s, 0]
                        if t == 0 and b == NB - 1:
                            pe.wait_ge(w_loaded, 3 * 16).then_inc(w_loaded, -3 * 16)
                        pe.wait_ge(freed[k], 1).then_inc(freed[k], -1)
                        nc.tensor.matmul(ring[k][:, 0:3 * P], xnT[:, (b + 1) % NB, P * t:P * t + P], w_now[:, :], start=True, stop=True).then_inc(to_act[k], 1)
                    if s[0] == "C":
                        _, g, vec = s
                        k = bank[s, 0]
                        if vec == 0:
                            pe.wait_ge(normed, 1).then_inc(normed, -1)
                        pe.wait_ge(freed[k], 1).then_inc(freed[k], -1)
                        for t in range(4):
                            ins = nc.tensor.transpose(ring[k][:, P * t:P * t + P], unit[g][:, t, vec, :, :], ident[:, :])
                        ins.then_inc(to_act[k], 1)
                    if s[0] == "NULL":
                        g = s[1]
                        k = bank[s, 0]
                        if g == 0 and b == NB - 1:
                            pe.wait_ge(null_loaded, 1).then_inc(null_loaded, -1)
                        pe.wait_ge(freed[k], 1).then_inc(freed[k], -1)
                        for t in range(4):
                            for h in range(2):
                                o = ring[k][:, 4 * t + 2 * h:4 * t + 2 * h + 2]
                                query = qT[n][:, h, P * (4 * g + t):P * (4 * g + t) + P]
                                nc.tensor.matmul(o, query, null_now[:, 0, h, :], start=True, stop=False)
                                ins = nc.tensor.matmul(o, query, null_now[:, 1, h, :], start=False, stop=True)
                        ins.then_inc(to_dve[k], 1)

            for k in range(RING):
                pe.sem_inc(freed[k], 1)
            for h in range(2):
                pe.sem_inc(score_free[h], 1)
            pe.wait_ge(zeroed, 2)
            pe.sem_inc(rtotal_ready, 1)
            turns(pe, run)
            for k in range(RING):
                pe.wait_ge(freed[k], 1)
            for b in range(NB):
                for g in range(2):
                    nc.tensor.transpose(ring[0][:, 0:P], null_all[:, b, 4 * g:4 * g + 4, :], ident[:, :]).then_inc(to_act[0], 1)
                    pe.wait_ge(nullT_ready, 1).then_inc(nullT_ready, -1)
                    pe.wait_ge(freed[1], 1).then_inc(freed[1], -1)
                    nc.tensor.matmul(ring[1][:, :], nullT, nvo[:, :, :], start=True, stop=True).then_inc(to_dve[1], 1)

        @block.scalar
        def _(act):
            def run(steps, hp, b):
                n = (b + 1) % 2
                for s in steps:
                    if s[0] == "T" and s[2] == 0:
                        t = s[1]
                        for g in range(1 + (t >= 4)):
                            k = bank[s, g]
                            c, e = 4 * P * g, min(4 * P * (g + 1), P * (t + 1))
                            act.wait_ge(to_act[k], 1).then_inc(to_act[k], -1)
                            nc.scalar.copy(probT[t % 2][:, 0, c:e], ring[k][:, 0:e - c]).then_inc(freed[k], 1)
                    if s[0] == "SM":
                        _, t, h = s
                        p = prob[t % 2][:, h, 0:P * (t + 1)]
                        act.wait_ge(shifted[h], 1).then_inc(shifted[h], -1)
                        act.sem_inc(score_free[h], 1)
                        nc.scalar.activation(p, p, ACT.Exp, bias=neg_max[:, t, h:h + 1], scale=-1.0, accum_out=row_sum[:, t, h:h + 1]).then_inc(prob_ready[h], 1)
                    if s[0] == "R1":
                        act.wait_ge(null_arg_ready, 1).then_inc(null_arg_ready, -1)
                        nc.scalar.activation(null_prob[:, :, :, :], null_arg[:, :, :, :], ACT.Exp).then_inc(null_prob_ready, 1)
                    if s[0] == "O":
                        act.wait_ge(o_full, 1).then_inc(o_full, -1)
                        nc.scalar.copy(oT[:, :], outT[:, :]).then_inc(o_copied, 1)
                    if s[0] == "PROJ":
                        k = bank[s, 0]
                        act.wait_ge(to_act[k], 1).then_inc(to_act[k], -1)
                        if s[1] % 4 == 3:
                            nc.scalar.copy(qkv[n][:, s[1], 0:QK], ring[k][:, 0:QK]).then_inc(projected, 1)
                            nc.scalar.copy(qkv[n][:, s[1], QK:3 * P], ring[k][:, QK:3 * P]).then_inc(freed[k], 1)
                        else:
                            nc.scalar.copy(qkv[n][:, s[1], :], ring[k][:, 0:3 * P]).then_inc(freed[k], 1)
                        if s[1] == NT - 1 and b == NB - 2:
                            act.sem_inc(w_free, 1)
                    if s[0] == "C":
                        _, g, vec = s
                        k = bank[s, 0]
                        act.wait_ge(to_act[k], 1).then_inc(to_act[k], -1)
                        if vec == 3:
                            act.sem_inc(unit_free, 1)
                        high = (qT, khT)[vec // 2][n][:, vec % 2, 4 * P * g:4 * P * g + 4 * P]
                        nc.scalar.activation(high, ring[k][:, :], ACT.Copy, scale=1.0 if vec < 2 else scales[:, 0:1]).then_inc(high_ready, 1)

            act.sem_inc(unit_free, 2)
            turns(act, run)
            for b in range(NB):
                for g in range(2):
                    act.wait_ge(to_act[0], 1).then_inc(to_act[0], -1)
                    nc.scalar.copy(nullT, ring[0][:, 0:P]).then_inc(nullT_ready, 1)

        @block.vector
        def _(dve):
            def run(steps, hp, b):
                r, n = b % 2, (b + 1) % 2
                for s in steps:
                    if s[0] == "T" and s[2] == 1:
                        t = s[1]
                        for g in range(1 + (t >= 4)):
                            k = bank[s, g]
                            c, e = 4 * P * g, min(4 * P * (g + 1), P * (t + 1))
                            dve.wait_ge(to_dve[k], 1).then_inc(to_dve[k], -1)
                            nc.vector.tensor_copy(probT[t % 2][:, 1, c:e], ring[k][:, 0:e - c]).then_inc(freed[k], 1)
                    if s[0] == "SM":
                        _, t, h = s
                        w, q = P * (t + 1), r if t else n
                        dve.wait_ge(score_full[h], 1).then_inc(score_full[h], -1)
                        nc.vector.tensor_tensor_reduce(out=prob[t % 2][:, h, 0:w], in0=score[h][:, 0:w], in1=table[:, h, FAR - P * t:FAR + P], scale=-1.0, scalar=null_min[q][:, t, h:h + 1], op0=ALU.add, op1=ALU.min, accum_out=neg_max[:, t, h:h + 1]).then_inc(shifted[h], 1)
                    if s[0] == "R1":
                        g = 4 * s[1]
                        nc.vector.tensor_tensor(null_arg[:, :, :, :], neg_max[:, g:g + 4, :].unsqueeze(3).to_broadcast([P, 4, 2, NULL]), null_neg[r][:, g:g + 4, :, :], ALU.subtract).then_inc(null_arg_ready, 1)
                    if s[0] == "R2":
                        g = 4 * s[1]
                        dve.wait_ge(null_prob_ready, 1).then_inc(null_prob_ready, -1)
                        nc.vector.tensor_reduce(total[:, :, :], null_prob[:, :, :, :], AX.X, ALU.add).then_inc(step, 1)
                        dve.wait_ge(step, 1).then_inc(step, -1)
                        nc.vector.tensor_tensor(total[:, :, :], total[:, :, :], row_sum[:, g:g + 4, :], ALU.add).then_inc(step, 1)
                        dve.wait_ge(step, 1).then_inc(step, -1)
                        nc.vector.reciprocal(rtotal[:, :, :], total[:, :, :]).then_inc(step, 1)
                        dve.wait_ge(step, 1).then_inc(step, -1)
                        nc.vector.tensor_copy(rtotal_wide[:, :, :, :], rtotal[:, :, :].unsqueeze(3).to_broadcast([P, 4, 2, DH]))
                        nc.vector.tensor_tensor(null_all[:, b:b + 1, g:g + 4, bass.ds(4 * hp, 4)].rearrange("p a t (h c) -> p (a t) h c", h=2), null_prob[:, :, :, :], rtotal[:, :, :].unsqueeze(3).to_broadcast([P, 4, 2, NULL]), ALU.mult).then_inc(rtotal_ready, 1)
                    if s[0] == "RB":
                        k = bank[s, 0]
                        dve.wait_ge(to_dve[k], 1).then_inc(to_dve[k], -1)
                        dve.wait_ge(o_copied, 1).then_inc(o_copied, -1)
                        nc.vector.tensor_tensor(oT[:, :], oT[:, :], ring[k][:, :], ALU.mult).then_inc(freed[k], 1)
                    if s[0] == "Y":
                        k = bank[s, 0]
                        batch = b if s[1] == 0 else (b - 1) % NB
                        dve.wait_ge(to_dve[k], 1).then_inc(to_dve[k], -1)
                        tiles = x[:, batch * NT + 4 * s[1]:batch * NT + 4 * s[1] + 4, :]
                        nc.vector.tensor_tensor(tiles, tiles, ring[k][:, :].rearrange("p (t d) -> p t d", t=4), ALU.add).then_inc(freed[k], 1)
                    if s[0] == "RS":
                        dve.wait_ge(squared, 1).then_inc(squared, -1)
                        nc.vector.tensor_reduce(norm2[:, :, :], square[:, :, :, :], AX.X, ALU.add).then_inc(step, 1)
                        dve.wait_ge(step, 1).then_inc(step, -1)
                        nc.vector.tensor_scalar(norm2[:, :, :], norm2[:, :, :], 1e-24, None, ALU.max).then_inc(summed, 1)
                    if s[0] == "C":
                        _, g, vec = s
                        k = bank[s, 0]
                        c = slice(4 * P * g, 4 * P * g + 4 * P)
                        dve.wait_ge(high_ready, 1).then_inc(high_ready, -1)
                        if vec < 2:
                            nc.vector.tensor_tensor(qT[n][DH:P, vec, c], ring[k][DH:P, :], qT[n][DH:P, vec, c].bitcast(F32), ALU.subtract).then_inc(freed[k], 1)
                        else:
                            nc.vector.scalar_tensor_tensor(klT[n][:, vec - 2, c], ring[k][:, :], scales[:, 0:1], khT[n][:, vec - 2, c].bitcast(F32), ALU.mult, ALU.subtract).then_inc(freed[k], 1)
                    if s[0] == "SLOPE" and b == NB - 1:
                        nc.vector.tensor_copy(null_now[:, :, :, :].unsqueeze(1), null_keys[:, bass.ds(hp + 1, 1), :, :, :].bitcast(F32)).then_inc(null_loaded, 1)
                        nc.vector.tensor_copy(slope_now[:, :], slope[:, bass.ds(2 * (hp + 1), 2)]).then_inc(step, 1)
                        dve.wait_ge(step, 1).then_inc(step, -1)
                    if s[0] == "TAB" and b == NB - 1:
                        nc.vector.tensor_scalar(table[:, s[1], :], dist[:, :], slope_now[:, s[1]:s[1] + 1], None, ALU.mult).then_inc(step, 1)
                        dve.wait_ge(step, 1).then_inc(step, -1)
                    if s[0] == "NULL":
                        k = bank[s, 0]
                        g = slice(4 * s[1], 4 * s[1] + 4)
                        dve.wait_ge(to_dve[k], 1).then_inc(to_dve[k], -1)
                        o = ring[k][:, 0:4 * 4].rearrange("p (t h c) -> p t h c", h=2, c=NULL)
                        for h in range(2):
                            ins = nc.vector.scalar_tensor_tensor(null_neg[n][:, g, h, :], null_dist[:, g, :], slope_now[:, h:h + 1], o[:, :, h, :], ALU.mult, ALU.subtract)
                        ins.then_inc(step, 1)
                        dve.wait_ge(step, 1).then_inc(step, -1)
                        nc.vector.tensor_reduce(null_min[n][:, g, :], null_neg[n][:, g, :, :], AX.X, ALU.min).then_inc(step, 1)
                        dve.wait_ge(step, 1).then_inc(step, -1)
                        dve.sem_inc(freed[k], 1)

            nc.vector.memset(outT[:, :], 0.0).then_inc(zeroed, 1)
            turns(dve, run)
            for b in range(NB):
                for g in range(2):
                    dve.wait_ge(to_dve[1], 1).then_inc(to_dve[1], -1)
                    tiles = x[:, b * NT + 4 * g:b * NT + 4 * g + 4, :]
                    nc.vector.tensor_tensor(tiles, tiles, ring[1][:, :].rearrange("p (t d) -> p t d", t=4), ALU.add).then_inc(freed[1], 1)


def build(nc, args, out):
    (x_d, gamma, w_q, w_kv, null_kv, q_scale, k_scale, w_out, Wc, bc, W1, b1, W2, b2) = args
    with ExitStack() as ctx:
        sb = lambda n, s, d=F32: ctx.enter_context(nc.sbuf_tensor(n, s, d))
        sem = lambda n: ctx.enter_context(nc.semaphore(n))
        x = sb("x", [P, 32, P])
        ident = sb("ident", [P, P])
        x_loaded = sem("x_loaded")
        ident_zero = sem("ident_zero")
        ident_made = sem("ident_made")
        stored = sem("stored")
        xv = x_d.rearrange("b (t p) d -> p (b t) d", p=P)
        ov = out.rearrange("b (t p) d -> p (b t) d", p=P)
        with nc.Block("start") as block:
            @block.sync
            def _(sp):
                sp.dma_start(x[:, :, :], xv).then_inc(x_loaded, 16)
                sp.wait_ge(x_loaded, 16)

            @block.gpsimd
            def _(pool):
                nc.gpsimd.memset(ident[:, :], 0.0).then_inc(ident_zero, 1)
                pool.wait_ge(ident_zero, 1)
                nc.gpsimd.affine_select(out=ident[:, :], in_=ident[:, :], compare_op=ALU.not_equal, fill=1.0, base=0, pattern=[[-1, P]], channel_multiplier=1).then_inc(ident_made, 1)
                pool.wait_ge(ident_made, 1)
        ffn(nc, x, ident, (Wc, bc, W1, b1, W2, b2), "f1_")
        attention(nc, x, ident, (gamma, w_q, w_kv, null_kv, q_scale, k_scale, w_out))
        ffn(nc, x, ident, (Wc, bc, W1, b1, W2, b2), "f2_")
        with nc.Block("end") as block:
            @block.sync
            def _(sp):
                sp.dma_start(ov, x[:, :, :]).then_inc(stored, 16)
                sp.wait_ge(stored, 16)


_INS = ['L0_attn_x', 'L0_attn_gamma', 'L0_attn_w_q', 'L0_attn_w_kv', 'L0_attn_null_kv', 'L0_attn_q_scale',
        'L0_attn_k_scale', 'L0_attn_w_out', 'L0_ffn_Wc', 'L0_ffn_bc', 'L0_ffn_W1', 'L0_ffn_b1', 'L0_ffn_W2', 'L0_ffn_b2']


def kernel(**inputs):
    import numpy as np
    import concourse.bacc as bacc
    from concourse.bass_utils import run_bass_kernel_spmd

    nc = bacc.Bacc("TRN2", target_bir_lowering=False, num_devices=1)
    arrays, args = {}, []
    for name in _INS:
        a = np.ascontiguousarray(inputs[name])
        arrays[f"in_{name}"] = a
        args.append(nc.dram_tensor(f"in_{name}", a.shape, mybir.dt.from_np(a.dtype), kind="ExternalInput").ap())
    out = nc.dram_tensor("out_x", inputs['L0_attn_x'].shape, F32, kind="ExternalOutput").ap()
    build(nc, args, out)
    r = run_bass_kernel_spmd(nc, [arrays], core_ids=[0])
    return r.results[0]["out_x"]
```

```python
from contextlib import ExitStack

import concourse.bass as bass
from concourse import mybir

F32 = mybir.dt.float32
F32R = mybir.dt.float32r
I32 = mybir.dt.int32
ALU = mybir.AluOpType
ACT = mybir.ActivationFunctionType
AX = mybir.AxisListType
P = 128
EPS = 1e-5


def newton_rsqrt(ops, eng, step, out, v, tmp):
    bits = out.bitcast(I32)
    ops.tensor_scalar(bits, v.bitcast(I32), -0.5, float(0x5F3759DF), ALU.mult, ALU.add).then_inc(step, 1)
    eng.wait_ge(step, 1).then_inc(step, -1)
    for _ in range(3):
        ops.tensor_tensor(tmp, out, out, ALU.mult).then_inc(step, 1)
        eng.wait_ge(step, 1).then_inc(step, -1)
        ops.tensor_tensor(tmp, tmp, v, ALU.mult).then_inc(step, 1)
        eng.wait_ge(step, 1).then_inc(step, -1)
        ops.tensor_scalar(tmp, tmp, -0.5, 1.5, ALU.mult, ALU.add).then_inc(step, 1)
        eng.wait_ge(step, 1).then_inc(step, -1)
        ops.tensor_tensor(out, tmp, out, ALU.mult).then_inc(step, 1)
        eng.wait_ge(step, 1).then_inc(step, -1)


def tile_stats(nc, dve, step, src, first, bn, mv, mean, var):
    for k in range(8):
        ins = nc.vector.bn_stats(bn[:, k, :], src[:, bass.ds(first + k, 1), :])
    ins.then_inc(step, 1)
    dve.wait_ge(step, 1).then_inc(step, -1)
    for k in range(8):
        ins = nc.vector.bn_aggr(mv[:, k, :], bn[:, k, :])
    ins.then_inc(step, 1)
    dve.wait_ge(step, 1).then_inc(step, -1)
    nc.vector.tensor_copy(mean[:, bass.ds(first, 8)], mv[:, :, 0])
    nc.vector.tensor_copy(var[:, bass.ds(first, 8)], mv[:, :, 1]).then_inc(step, 1)
    dve.wait_ge(step, 1).then_inc(step, -1)


def ffn(nc, x, ident, dram, pre):
    Wc, bc, W1, b1, W2, b2 = dram
    NE, NS, _, F = W1.shape
    ES = NE * NS
    TILES = x.shape[1]
    GROUP = 32
    PER = P // GROUP
    NG = TILES * PER
    with ExitStack() as ctx:
        sb = lambda n, s, d=F32: ctx.enter_context(nc.sbuf_tensor(pre + n, s, d))
        pb = lambda n: ctx.enter_context(nc.psum_tensor(pre + n, [P, 4 * P], F32))
        signals = []

        def sem(n):
            signals.append(nc.alloc_semaphore(pre + n))
            return signals[-1]


        G = sb("G", [P, ES, NG])
        permT = sb("permT", [P, TILES, P])
        bn = sb("bn", [P, 8, 6])
        mv = sb("mv", [P, 8, 2])
        mean = sb("mean", [P, TILES])
        var = sb("var", [P, TILES])
        rstd = sb("rstd", [P, TILES])
        tmp = sb("tmp", [P, TILES])
        wc = sb("wc", [P, ES])
        bcol = sb("bcol", [P, 1])
        tie = sb("tie", [P, 4 * P])
        tie_i = sb("tie_i", [P, 4 * P], I32)
        b1r = sb("b1r", [NE, NS * F])
        b2r = sb("b2r", [ES, P])
        b1T = sb("b1T", [P, NE])
        b2T = sb("b2T", [P, ES])
        z = [sb(f"z{k}", [P, 4, P]) for k in range(2)]
        zT = sb("zT", [P, 4 * P])
        L = sb("L", [P, 4 * P])
        top = sb("top", [P, 16])
        pT4 = sb("pT4", [P, 4, P])

        ps = [pb(f"ps{i}") for i in range(8)]

        loaded = sem("loaded")
        iota_done = sem("iota_done")
        step = sem("step")
        pool_step = sem("pool_step")
        rstd_ready = sem("rstd_ready")
        setup_full = sem("setup_full")
        setup_done = sem("setup_done")
        z_ready = [sem(f"z_ready{k}") for k in range(2)]
        z_for_pe = [sem(f"z_for_pe{k}") for k in range(2)]
        z_turned = [sem(f"z_turned{k}") for k in range(2)]
        z_split = [sem(f"z_split{k}") for k in range(2)]
        split_free = [sem(f"split_free{k}") for k in range(2)]
        zT_full = sem("zT_full")
        zT_ready = sem("zT_ready")
        logits = sem("logits")
        perm_ready = sem("perm_ready")
        perm_full = sem("perm_full")
        perm_for_dve = sem("perm_for_dve")
        half_taken = sem("half_taken")
        taken_ready = [sem(f"taken_ready{k}") for k in range(2)]
        g_full = [sem(f"g_full{t}") for t in range(4)]
        g_free = [sem(f"g_free{t}") for t in range(4)]

        with ExitStack() as select:
            sb1 = lambda n, s, d=F32: select.enter_context(nc.sbuf_tensor(pre + n, s, d))
            zh = [sb1(f"zh{k}", [P, 4, P], F32R) for k in range(2)]
            zl = [sb1(f"zl{k}", [P, 4, P], F32R) for k in range(2)]
            taken = [sb1(f"taken{k}", [P, 4, PER, P], F32R) for k in range(2)]
            zero = sb1("zero", [P, P])
            zero_ready = sem("zero_ready")
            taken_zero = sem("taken_zero")
            block = select.enter_context(nc.Block(pre + "select"))

            @block.sync
            def _(sp):
                sp.dma_start(wc[:, :], Wc.rearrange("d e s -> d (e s)")).then_inc(loaded, 16)
                sp.dma_start(bcol[:, :], bc.rearrange("e s -> (e s)").unsqueeze(1)).then_inc(loaded, 16)
                sp.dma_start(b1r[:, :], b1.rearrange("e s f -> e (s f)")).then_inc(loaded, 16)
                sp.dma_start(b2r[:, :], b2.rearrange("e s d -> (e s) d")).then_inc(loaded, 16)

            @block.gpsimd
            def _(pool):
                nc.gpsimd.iota(tie_i[:, :], [[0, 16], [1, GROUP]], base=0, channel_multiplier=0).then_inc(iota_done, 1)
                nc.gpsimd.memset(zero[:, :], 0.0).then_inc(zero_ready, 1)
                pool.wait_ge(zero_ready, 1)
                for k in range(2):
                    ins = nc.gpsimd.tensor_copy(taken[k][:, :, :, :].rearrange("p t g e -> p (t g) e"), zero[:, :].unsqueeze(1).to_broadcast([P, 4 * PER, P]))
                ins.then_inc(taken_zero, 1)
                pool.wait_ge(rstd_ready, 1)
                with pool.Fori(0, TILES // 8) as i:
                    for k in range(2):
                        four = bass.ds(8 * i + 4 * k, 4)
                        pool.wait_ge(z_turned[k], 1).then_inc(z_turned[k], -1)
                        pool.wait_ge(z_split[k], 1).then_inc(z_split[k], -1)
                        nc.gpsimd.tensor_tensor(z[k][:, :, :], x[:, four, :], mean[:, four].unsqueeze(2).to_broadcast([P, 4, P]), ALU.subtract).then_inc(pool_step, 1)
                        pool.wait_ge(pool_step, 1).then_inc(pool_step, -1)
                        nc.gpsimd.tensor_tensor(z[k][:, :, :], z[k][:, :, :], rstd[:, four].unsqueeze(2).to_broadcast([P, 4, P]), ALU.mult).then_inc(pool_step, 1)
                        pool.wait_ge(pool_step, 1).then_inc(pool_step, -1)
                        pool.sem_inc(z_ready[k], 1)
                        pool.sem_inc(z_for_pe[k], 1)

            @block.tensor
            def _(pe):
                pe.wait_ge(loaded, 64)
                nc.tensor.transpose(ps[7][:, 0:NE], b1r[:, :], ident[0:NE, 0:NE])
                nc.tensor.transpose(ps[7][:, P:P + ES], b2r[:, :], ident[:, :]).then_inc(setup_full, 1)

                def gather(k, first):
                    if first == 0:
                        pe.wait_ge(taken_ready[k], 1).then_inc(taken_ready[k], -1)
                        pe.wait_ge(half_taken, 1).then_inc(half_taken, -1)
                    for t in (first, first + 1):
                        pe.wait_ge(g_free[t], 1).then_inc(g_free[t], -1)
                        nc.tensor.matmul(ps[3 + t][:, :], zh[k][:, t, :], taken[k][:, t, :, :], start=True, stop=False)
                        nc.tensor.matmul(ps[3 + t][:, :], zl[k][:, t, :], taken[k][:, t, :, :], start=False, stop=True).then_inc(g_full[t], 1)

                def select(k, taking):
                    pe.wait_ge(z_for_pe[k], 1).then_inc(z_for_pe[k], -1)
                    for t in range(4):
                        ins = nc.tensor.transpose(ps[0][:, P * t:P * t + P], z[k][:, t, :], ident[:, :])
                    ins.then_inc(zT_full, 1)
                    if taking:
                        gather(1 - k, 0)
                    pe.wait_ge(zT_ready, 1).then_inc(zT_ready, -1)
                    nc.tensor.matmul(ps[1][:, :], wc[:, :], zT[:, :], start=True, stop=True).then_inc(logits, 1)
                    if taking:
                        gather(1 - k, 2)
                    pe.wait_ge(perm_ready, 1).then_inc(perm_ready, -1)
                    for t in range(4):
                        ins = nc.tensor.transpose(ps[2][:, P * t:P * t + P], pT4[:, t, :], ident[:, :])
                    ins.then_inc(perm_full, 1)

                select(0, False)
                with pe.Fori(0, TILES // 8 - 1) as i:
                    for k in range(2):
                        select(1 - k, True)
                select(1, True)
                gather(1, 0)
                gather(1, 2)

            @block.scalar
            def _(act):
                act.wait_ge(setup_full, 1)
                nc.scalar.copy(b1T[:, :], ps[7][:, 0:NE])
                nc.scalar.copy(b2T[:, :], ps[7][:, P:P + ES]).then_inc(setup_done, 1)
                act.wait_ge(setup_done, 1)
                for t in range(4):
                    act.sem_inc(g_free[t], 1)
                for k in range(2):
                    act.sem_inc(z_turned[k], 1)
                    act.sem_inc(z_split[k], 1)
                    act.sem_inc(split_free[k], 1)

                def gathered(n, k):
                    for t in range(4):
                        act.wait_ge(g_full[t], 1).then_inc(g_full[t], -1)
                        if t == 3:
                            act.sem_inc(split_free[k], 1)
                        nc.scalar.copy(G[:, :, bass.ds((n * 4 + t) * PER, PER)], ps[3 + t][:, :].rearrange("p (g e) -> p e g", g=PER)).then_inc(g_free[t], 1)

                def select(k, before):
                    act.wait_ge(zT_full, 1).then_inc(zT_full, -1)
                    act.sem_inc(z_turned[k], 1)
                    nc.scalar.copy(zT[:, :], ps[0][:, :]).then_inc(zT_ready, 1)
                    if before is not None:
                        gathered(before, 1 - k)
                    act.wait_ge(perm_full, 1).then_inc(perm_full, -1)
                    act.sem_inc(perm_for_dve, 1)
                    for g in range(PER // 2):
                        rows = slice(GROUP * g, GROUP * g + GROUP)
                        ins = nc.scalar.copy(taken[k][rows, :, g, :], ps[2][rows, :].rearrange("p (t e) -> p t e", t=4))
                    ins.then_inc(taken_ready[k], 1)

                act.wait_ge(taken_zero, 1)
                LAST = TILES // 4 - 1
                select(0, None)
                with act.Fori(0, TILES // 8 - 1) as i:
                    for k in range(2):
                        select(1 - k, 2 * i + k)
                select(1, LAST - 1)
                gathered(LAST, 1)

            @block.vector
            def _(dve):
                dve.wait_ge(iota_done, 1)
                nc.vector.tensor_scalar(tie[:, :], tie_i[:, :], 1e-6 / (GROUP - 1), None, ALU.mult).then_inc(step, 1)
                dve.wait_ge(step, 1).then_inc(step, -1)
                with dve.Fori(0, TILES // 8) as i:
                    tile_stats(nc, dve, step, x, i * 8, bn, mv, mean, var)
                nc.vector.tensor_scalar(var[:, :], var[:, :], EPS, None, ALU.add).then_inc(step, 1)
                dve.wait_ge(step, 1).then_inc(step, -1)
                newton_rsqrt(nc.vector, dve, step, rstd[:, :], var[:, :], tmp[:, :])
                dve.sem_inc(rstd_ready, 1)
                dve.wait_ge(loaded, 64)

                def split(k):
                    dve.wait_ge(z_ready[k], 1).then_inc(z_ready[k], -1)
                    dve.wait_ge(split_free[k], 1).then_inc(split_free[k], -1)
                    nc.vector.tensor_copy(zh[k][:, :, :], z[k][:, :, :]).then_inc(step, 1)
                    dve.wait_ge(step, 1).then_inc(step, -1)
                    nc.vector.tensor_tensor(zl[k][:, :, :], z[k][:, :, :], zh[k][:, :, :].bitcast(F32), ALU.subtract).then_inc(z_split[k], 1)

                def choose(n, k, ahead):
                    dve.wait_ge(logits, 1).then_inc(logits, -1)
                    nc.vector.scalar_tensor_tensor(L[:, :], ps[1][:, :], bcol[:, 0:1], tie[:, :], ALU.add, ALU.add).then_inc(step, 1)
                    dve.wait_ge(step, 1).then_inc(step, -1)
                    nc.vector.tensor_reduce(top[:, :], L[:, :].rearrange("p (n t) -> p n t", t=GROUP), AX.X, ALU.max).then_inc(step, 1)
                    dve.wait_ge(step, 1).then_inc(step, -1)
                    nc.vector.tensor_tensor(pT4[:, :, :].rearrange("p a (n t) -> p (a n) t", t=GROUP), L[:, :].rearrange("p (n t) -> p n t", t=GROUP), top[:, :].unsqueeze(2).to_broadcast([P, 16, GROUP]), ALU.is_equal).then_inc(step, 1)
                    dve.wait_ge(step, 1).then_inc(step, -1)
                    dve.sem_inc(perm_ready, 1)
                    nc.vector.tensor_copy(permT[:, bass.ds(4 * n, 4), :], pT4[:, :, :]).then_inc(step, 1)
                    dve.wait_ge(step, 1).then_inc(step, -1)
                    dve.wait_ge(perm_for_dve, 1).then_inc(perm_for_dve, -1)
                    for g in range(PER // 2, PER):
                        rows = slice(GROUP * g, GROUP * g + GROUP)
                        ins = nc.vector.tensor_copy(taken[k][rows, :, g, :], ps[2][rows, :].rearrange("p (t e) -> p t e", t=4))
                    ins.then_inc(half_taken, 1)
                    if ahead is not None:
                        split(ahead)

                dve.wait_ge(taken_zero, 1)
                split(0)
                with dve.Fori(0, TILES // 8 - 1) as i:
                    for k in range(2):
                        choose(2 * i + k, k, 1 - k)
                choose(TILES // 4 - 2, 0, 1)
                choose(TILES // 4 - 1, 1, None)

        R = sb("R", [P, NG, ES])
        with ExitStack() as experts:
            sb2 = lambda n, s, d=F32: experts.enter_context(nc.sbuf_tensor(pre + n, s, d))
            w1 = [sb2(f"w1_{j}", [P, 4, NS, F]) for j in range(2)]
            w2 = [sb2(f"w2_{j}", [P, 4, NS, F]) for j in range(2)]
            w2T = [sb2(f"w2T{j}", [P, 4, P]) for j in range(2)]
            b1e = [sb2(f"b1e{j}", [P, 4]) for j in range(2)]
            g_now = [sb2(f"g_now{k}", [P, NS, NG]) for k in range(4)]
            hb = [sb2(f"hb{k}", [P, NS, NG]) for k in range(4)]
            w_loaded = [sem(f"w_loaded{j}") for j in range(2)]
            w_free = [sem(f"w_free{j}") for j in range(2)]
            w2_full = sem("w2_full")
            w2T_ready = sem("w2T_ready")
            b1e_ready = sem("b1e_ready")
            g_copied = sem("g_copied")
            g_now_free = sem("g_now_free")
            h_full = sem("h_full")
            hb_zero = sem("hb_zero")
            hb_ready = sem("hb_ready")
            r_full = sem("r_full")
            r_free = sem("r_free")
            block = experts.enter_context(nc.Block(pre + "experts"))

            @block.sync
            def _(sp):
                with sp.Fori(0, NE // 8) as i:
                    for j in range(2):
                        sp.wait_ge(w_free[j], 1).then_inc(w_free[j], -1)
                        for dst, src in ((w1[j], W1), (w2[j], W2)):
                            for k in range(4):
                                sp.dma_start(dst[:, k, :, :], src[bass.ds(8 * i + 4 * j + k, 1)].rearrange("a s d f -> d (a s) f")).then_inc(w_loaded[j], 16)

            @block.tensor
            def _(pe):
                def result(k):
                    pe.wait_ge(r_free, 1).then_inc(r_free, -1)
                    nc.tensor.matmul(ps[4 + k % 4][:, :], w2T[k // 4][:, k % 4, :], hb[k % 4][:, :, :], start=True, stop=True).then_inc(r_full, 1)

                pe.wait_ge(hb_zero, 1)
                with pe.Fori(0, NE // 8) as i:
                    for k in range(8):
                        j = k // 4
                        if k % 4 == 0:
                            pe.wait_ge(w_loaded[j], 8 * 16).then_inc(w_loaded[j], -8 * 16)
                            for n in range(4):
                                ins = nc.tensor.transpose(ps[j][:, P * n:P * n + P], w2[j][:, n, :, :], ident[:, :])
                            ins.then_inc(w2_full, 1)
                        pe.wait_ge(g_copied, 1).then_inc(g_copied, -1)
                        if k > 1:
                            pe.wait_ge(hb_ready, 1).then_inc(hb_ready, -1)
                        for s in range(NS):
                            ins = nc.tensor.matmul(ps[2 + k % 2][F * s:F * s + F, 0:NG], w1[j][:, k % 4, s, :], g_now[k % 4][:, s, :], start=True, stop=True)
                        ins.then_inc(h_full, 1)
                        if k % 4 == 2:
                            pe.wait_ge(w2T_ready, 1).then_inc(w2T_ready, -1)
                        if k > 1:
                            result(k - 2)
                    for k in (6, 7):
                        pe.wait_ge(hb_ready, 1).then_inc(hb_ready, -1)
                        result(k)

            @block.scalar
            def _(act):
                for j in range(2):
                    act.sem_inc(w_free[j], 1)
                    act.sem_inc(g_now_free, 2)
                act.sem_inc(r_free, 4)
                act.wait_ge(hb_zero, 1)
                with act.Fori(0, NE // 8) as i:
                    for k in range(8):
                        j = k // 4
                        if k % 4 == 0:
                            act.wait_ge(w2_full, 1).then_inc(w2_full, -1)
                            nc.scalar.copy(w2T[j][:, :, :], ps[j][:, :].rearrange("p (n d) -> p n d", n=4)).then_inc(w2T_ready, 1)
                            nc.scalar.copy(b1e[j][:, :], b1T[:, bass.ds(8 * i + 4 * j, 4)]).then_inc(b1e_ready, 1)
                            act.wait_ge(b1e_ready, 1).then_inc(b1e_ready, -1)
                        act.wait_ge(h_full, 1).then_inc(h_full, -1)
                        act.sem_inc(g_now_free, 1)
                        if k % 4 == 3:
                            act.sem_inc(w_free[j], 1)
                        for s in range(NS):
                            rows = slice(F * s, F * s + F)
                            ins = nc.scalar.activation(hb[k % 4][rows, s, :], ps[2 + k % 2][rows, 0:NG], ACT.Relu, bias=b1e[j][rows, k % 4:k % 4 + 1])
                        ins.then_inc(hb_ready, 1)

            @block.vector
            def _(dve):
                def add_bias(i, k):
                    dve.wait_ge(r_full, 1).then_inc(r_full, -1)
                    mine = bass.ds((8 * i + k) * NS, NS)
                    nc.vector.tensor_tensor(R[:, :, mine].rearrange("p n s -> p s n"), ps[4 + k % 4][:, :].rearrange("p (s n) -> p s n", s=NS), b2T[:, mine].unsqueeze(2).to_broadcast([P, NS, NG]), ALU.add).then_inc(r_free, 1)

                with dve.Fori(0, NE // 8) as i:
                    for k in range(8):
                        dve.wait_ge(g_now_free, 1).then_inc(g_now_free, -1)
                        nc.vector.tensor_copy(g_now[k % 4][:, :, :], G[:, bass.ds((8 * i + k) * NS, NS), :]).then_inc(g_copied, 1)
                        if k > 2:
                            add_bias(i, k - 3)
                    for k in range(5, 8):
                        add_bias(i, k)

            @block.gpsimd
            def _(pool):
                for k in range(4):
                    ins = nc.gpsimd.memset(hb[k][:, :, :], 0.0)
                ins.then_inc(hb_zero, 1)

        with ExitStack() as back:
            sb3 = lambda n, s, d=F32: back.enter_context(nc.sbuf_tensor(pre + n, s, d))
            Rs = [sb3(f"Rs{k}", [P, PER, ES]) for k in range(4)]
            Rt = [sb3(f"Rt{k}", [P, PER, P]) for k in range(4)]
            pT = [sb3(f"pT{k}", [P, 4, P]) for k in range(2)]
            rs_ready = sem("rs_ready")
            rs_free = sem("rs_free")
            pT_ready = sem("pT_ready")
            pT_free = sem("pT_free")
            rt_full = sem("rt_full")
            rt_ready = sem("rt_ready")
            y_full = sem("y_full")
            y_free = sem("y_free")
            block = back.enter_context(nc.Block(pre + "back"))

            @block.gpsimd
            def _(pool):
                with pool.Fori(0, TILES // 8) as i:
                    for k in range(2):
                        pool.wait_ge(pT_free, 1).then_inc(pT_free, -1)
                        nc.gpsimd.tensor_copy(pT[k][:, :, :], permT[:, bass.ds(8 * i + 4 * k, 4), :]).then_inc(pT_ready, 1)

            @block.tensor
            def _(pe):
                def give(k, t):
                    if t == 0:
                        pe.wait_ge(pT_ready, 1).then_inc(pT_ready, -1)
                        pe.wait_ge(y_free, 1).then_inc(y_free, -1)
                    pe.wait_ge(rt_ready, 1).then_inc(rt_ready, -1)
                    for g in range(PER):
                        rows = slice(GROUP * g, GROUP * g + GROUP)
                        ins = nc.tensor.matmul(ps[4 + k][rows, P * t:P * t + P], pT[k][:, t, rows], Rt[t][:, g, :], start=True, stop=True)
                    if t == 3:
                        ins.then_inc(y_full, 1)

                with pe.Fori(0, TILES // 8) as i:
                    for n in range(8):
                        k, t = n // 4, n % 4
                        pe.wait_ge(rs_ready, 1).then_inc(rs_ready, -1)
                        for g in range(PER):
                            ins = nc.tensor.transpose(ps[t][:, P * g:P * g + P], Rs[t][:, g, :], ident[:, :])
                        ins.then_inc(rt_full, 1)
                        if n > 1:
                            give((n - 2) // 4, (n - 2) % 4)
                    give(1, 2)
                    give(1, 3)

            @block.scalar
            def _(act):
                for k in range(2):
                    act.sem_inc(rs_free, 2)
                    act.sem_inc(pT_free, 1)
                    act.sem_inc(y_free, 1)
                with act.Fori(0, TILES // 8) as i:
                    for n in range(8):
                        act.wait_ge(rt_full, 1).then_inc(rt_full, -1)
                        act.sem_inc(rs_free, 1)
                        nc.scalar.copy(Rt[n % 4][:, :, :], ps[n % 4][:, :].rearrange("p (g d) -> p g d", g=PER)).then_inc(rt_ready, 1)

            @block.vector
            def _(dve):
                def add(i, k):
                    dve.wait_ge(y_full, 1).then_inc(y_full, -1)
                    dve.sem_inc(pT_free, 1)
                    tiles = x[:, bass.ds(8 * i + 4 * k, 4), :]
                    nc.vector.scalar_tensor_tensor(tiles, ps[4 + k][:, :].rearrange("p (t d) -> p t d", t=4), 0.5, tiles, ALU.mult, ALU.add).then_inc(y_free, 1)

                with dve.Fori(0, TILES // 8) as i:
                    for n in range(8):
                        dve.wait_ge(rs_free, 1).then_inc(rs_free, -1)
                        nc.vector.tensor_copy(Rs[n % 4][:, :, :], R[:, bass.ds((8 * i + n) * PER, PER), :]).then_inc(rs_ready, 1)
                        if n == 7:
                            add(i, 0)
                    add(i, 1)

        nc.all_engine_barrier()
        nc.clear_and_free_semaphores(signals)
        nc.all_engine_barrier()


def prepare_attention(nc, x, ident, dram, outs, slopes):
    gamma, w_q, w_kv, null_kv, q_scale, k_scale, w_out = dram
    xnT, wo, scales, dist, null_dist, slope, null_keys, nvo = outs
    TILES = x.shape[1]
    HP = wo.shape[1] - 1
    HEADS, _, DH = null_kv.shape
    ROWS = HEADS * 4
    NT = null_dist.shape[1]
    NB = TILES // NT
    FAR = dist.shape[1] - P
    with ExitStack() as ctx:
        sb = lambda n, s, d=F32: ctx.enter_context(nc.sbuf_tensor("p_" + n, s, d))
        sem = lambda n: ctx.enter_context(nc.semaphore("p_" + n))
        ps = [ctx.enter_context(nc.psum_tensor(f"p_ps{k}", [P, 4 * P], F32)) for k in range(5)]
        bn = sb("bn", [P, 8, 6])
        mv = sb("mv", [P, 8, 2])
        mean = sb("mean", [P, TILES])
        var = sb("var", [P, TILES])
        rstd = sb("rstd", [P, TILES])
        rstd2 = sb("rstd2", [P, TILES])
        tmp = sb("tmp", [P, TILES])
        zn = sb("zn", [P, 2, 4, P])
        gcol = sb("gcol", [P, 1])
        qs = sb("qs", [P, DH])
        ks = sb("ks", [P, DH])
        qs_col = sb("qs_col", [P, 1])
        ks_col = sb("ks_col", [P, 1])
        row_scales = sb("row_scales", [P, DH])
        identr = sb("identr", [P, P], F32R)
        nk = sb("nk", [ROWS, 2, DH])
        nsq = sb("nsq", [ROWS, DH])
        ns = sb("ns", [ROWS, 1])
        nr = sb("nr", [ROWS, 1])
        nt = sb("nt", [ROWS, 1])
        nkn = sb("nkn", [ROWS, 2, DH])
        nhi = sb("nhi", [ROWS, 2, DH], F32R)
        nlo = sb("nlo", [ROWS, 2, DH], F32R)
        nvb = sb("nvb", [P, HP, 4, 4 * HP])
        blk = sb("blk", [P, 4, P])
        dist_i = sb("dist_i", [P, FAR + P], I32)
        null_dist_i = sb("null_dist_i", [P, NT, 2], I32)

        loaded = sem("loaded")
        pool_step = sem("pool_step")
        iotas = sem("iotas")
        dist_float = sem("dist_float")
        masks = sem("masks")
        step = sem("step")
        null_split = sem("null_split")
        null_full = sem("null_full")
        nvb_ready = sem("nvb_ready")
        nvo_full = sem("nvo_full")
        zn_ready = [sem(f"zn_ready{k}") for k in range(2)]
        zT_full = [sem(f"zT_full{k}") for k in range(2)]
        zn_free = [sem(f"zn_free{k}") for k in range(2)]

        block = ctx.enter_context(nc.Block("prepare"))

        @block.sync
        def _(sp):
            sp.dma_start(gcol[:, :], gamma.unsqueeze(1)).then_inc(loaded, 16)
            sp.dma_start(qs[:, :], q_scale.unsqueeze(0).to_broadcast([P, DH])).then_inc(loaded, 16)
            sp.dma_start(ks[:, :], k_scale.unsqueeze(0).to_broadcast([P, DH])).then_inc(loaded, 16)
            for k in range(2):
                sp.dma_start(nk[:, k, :], null_kv.rearrange("h c d -> (h c) d")).then_inc(loaded, 16)
            for k in range(2):
                sp.dma_start(qs_col[DH * k:DH * k + DH, :], q_scale.unsqueeze(1)).then_inc(loaded, 16)
                sp.dma_start(ks_col[DH * k:DH * k + DH, :], k_scale.unsqueeze(1)).then_inc(loaded, 16)
            sp.dma_start(wo[:, 1:HP + 1, :], w_out.rearrange("(m p) n -> p m n", p=P)).then_inc(loaded, 16)
            sp.wait_ge(loaded, 10 * 16)

        @block.gpsimd
        def _(pool):
            nc.gpsimd.iota(dist_i[:, :], [[1, FAR + P]], base=-FAR, channel_multiplier=-1)
            nc.gpsimd.iota(null_dist_i[:, :, :], [[P, NT], [-1, 2]], base=2, channel_multiplier=1).then_inc(iotas, 1)
            nc.gpsimd.memset(blk[:, :, :], 1.0)
            nc.gpsimd.memset(nvb[:, :, :, :], 0.0)
            nc.gpsimd.memset(wo[:, 0:1, :], 0.0)
            for h, m in enumerate(slopes + slopes[0:2]):
                ins = nc.gpsimd.memset(slope[:, h:h + 1], float(m))
            ins.then_inc(pool_step, 1)
            pool.wait_ge(pool_step, 1).then_inc(pool_step, -1)
            nc.gpsimd.affine_select(out=blk[:, :, :], in_=blk[:, :, :], compare_op=ALU.is_ge, fill=0.0, base=0, pattern=[[-32, 4], [0, P]], channel_multiplier=1).then_inc(pool_step, 1)
            pool.wait_ge(pool_step, 1).then_inc(pool_step, -1)
            nc.gpsimd.affine_select(out=blk[:, :, :], in_=blk[:, :, :], compare_op=ALU.is_ge, fill=0.0, base=31, pattern=[[32, 4], [0, P]], channel_multiplier=-1).then_inc(masks, 1)
            pool.wait_ge(dist_float, 1).then_inc(dist_float, -1)
            nc.gpsimd.affine_select(out=dist[:, :], in_=dist[:, :], compare_op=ALU.is_ge, fill=-1e37, base=FAR, pattern=[[-1, FAR + P]], channel_multiplier=1).then_inc(pool_step, 1)
            pool.wait_ge(pool_step, 1)

        @block.tensor
        def _(pe):
            with pe.Fori(0, TILES // 8) as i:
                for k in range(2):
                    pe.wait_ge(zn_ready[k], 1).then_inc(zn_ready[k], -1)
                    for t in range(4):
                        ins = nc.tensor.transpose(ps[k][:, P * t:P * t + P], zn[:, k, t, :], ident[:, :])
                    ins.then_inc(zT_full[k], 1)
            pe.wait_ge(null_split, 1).then_inc(null_split, -1)
            nc.tensor.transpose(ps[2][:, 0:ROWS].bitcast(F32R), nhi[:, :, :], identr[0:ROWS, 0:ROWS])
            nc.tensor.transpose(ps[2][:, P:P + ROWS].bitcast(F32R), nlo[:, :, :], identr[0:ROWS, 0:ROWS])
            nc.tensor.transpose(ps[2][:, 2 * P:2 * P + ROWS], nk[:, :, :], ident[0:ROWS, 0:ROWS]).then_inc(null_full, 1)
            pe.wait_ge(nvb_ready, 1).then_inc(nvb_ready, -1)
            for m in range(HP):
                ins = nc.tensor.matmul(ps[3][:, 0:P], nvb[:, m, :, :], wo[:, m + 1, :], start=(m == 0), stop=(m == HP - 1))
            ins.then_inc(nvo_full, 1)

        @block.scalar
        def _(act):
            act.wait_ge(loaded, 10 * 16)
            for k in range(2):
                act.sem_inc(zn_free[k], 1)
            flat = xnT[:, :, :].rearrange("p b n -> p (b n)")
            with act.Fori(0, TILES // 8) as i:
                for k in range(2):
                    act.wait_ge(zT_full[k], 1).then_inc(zT_full[k], -1)
                    nc.scalar.activation(flat[:, bass.ds((2 * i + k) * 4 * P, 4 * P)], ps[k][:, :], ACT.Copy, scale=gcol[:, 0:1]).then_inc(zn_free[k], 1)

        @block.vector
        def _(dve):
            nc.vector.tensor_copy(identr[:, :], ident[:, :]).then_inc(step, 1)
            dve.wait_ge(step, 1).then_inc(step, -1)
            dve.wait_ge(iotas, 1)
            nc.vector.tensor_copy(dist[:, :], dist_i[:, :]).then_inc(step, 1)
            dve.wait_ge(step, 1).then_inc(step, -1)
            nc.vector.tensor_copy(null_dist[:, :, :], null_dist_i[:, :, :]).then_inc(dist_float, 1)
            with dve.Fori(0, TILES // 8) as i:
                tile_stats(nc, dve, step, x, i * 8, bn, mv, mean, var)
            nc.vector.tensor_scalar(rstd2[:, :], var[:, :], EPS, None, ALU.add).then_inc(step, 1)
            dve.wait_ge(step, 1).then_inc(step, -1)
            newton_rsqrt(nc.vector, dve, step, rstd[:, :], rstd2[:, :], tmp[:, :])
            for _ in range(2):
                nc.vector.tensor_tensor(var[:, :], var[:, :], rstd[:, :], ALU.mult).then_inc(step, 1)
                dve.wait_ge(step, 1).then_inc(step, -1)
            nc.vector.tensor_scalar(var[:, :], var[:, :], EPS, None, ALU.add).then_inc(step, 1)
            dve.wait_ge(step, 1).then_inc(step, -1)
            newton_rsqrt(nc.vector, dve, step, rstd2[:, :], var[:, :], tmp[:, :])
            nc.vector.tensor_tensor(rstd[:, :], rstd[:, :], rstd2[:, :], ALU.mult).then_inc(step, 1)
            dve.wait_ge(step, 1).then_inc(step, -1)
            with dve.Fori(0, TILES // 8) as i:
                for k in range(2):
                    four = bass.ds(8 * i + 4 * k, 4)
                    dve.wait_ge(zn_free[k], 1).then_inc(zn_free[k], -1)
                    nc.vector.tensor_tensor(zn[:, k, :, :], x[:, four, :], mean[:, four].unsqueeze(2).to_broadcast([P, 4, P]), ALU.subtract).then_inc(step, 1)
                    dve.wait_ge(step, 1).then_inc(step, -1)
                    nc.vector.tensor_tensor(zn[:, k, :, :], zn[:, k, :, :], rstd[:, four].unsqueeze(2).to_broadcast([P, 4, P]), ALU.mult).then_inc(zn_ready[k], 1)
            dve.wait_ge(loaded, 10 * 16)
            nc.vector.scalar_tensor_tensor(scales[:, :], qs_col[:, :], 8.0, ks_col[:, :], ALU.mult, ALU.mult)
            nc.vector.scalar_tensor_tensor(row_scales[:, :], qs[:, :], 8.0, ks[:, :], ALU.mult, ALU.mult).then_inc(step, 1)
            dve.wait_ge(step, 1).then_inc(step, -1)
            nc.vector.tensor_tensor(nsq[:, :], nk[:, 0, :], nk[:, 0, :], ALU.mult).then_inc(step, 1)
            dve.wait_ge(step, 1).then_inc(step, -1)
            nc.vector.tensor_reduce(ns[:, :], nsq[:, :], AX.X, ALU.add).then_inc(step, 1)
            dve.wait_ge(step, 1).then_inc(step, -1)
            nc.vector.tensor_scalar(ns[:, :], ns[:, :], 1e-24, None, ALU.max).then_inc(step, 1)
            dve.wait_ge(step, 1).then_inc(step, -1)
            newton_rsqrt(nc.vector, dve, step, nr[:, :], ns[:, :], nt[:, :])
            nc.vector.scalar_tensor_tensor(nkn[:, :, :], nk[:, :, :], nr[:, 0:1], row_scales[0:ROWS, :].unsqueeze(1).to_broadcast([ROWS, 2, DH]), ALU.mult, ALU.mult).then_inc(step, 1)
            dve.wait_ge(step, 1).then_inc(step, -1)
            nc.vector.tensor_copy(nhi[:, :, :], nkn[:, :, :]).then_inc(step, 1)
            dve.wait_ge(step, 1).then_inc(step, -1)
            nc.vector.tensor_tensor(nlo[:, :, :], nkn[:, :, :], nhi[:, :, :].bitcast(F32), ALU.subtract).then_inc(null_split, 1)
            dve.wait_ge(null_full, 1).then_inc(null_full, -1)
            for part in range(2):
                keys = ps[2][:, P * part:P * part + ROWS].rearrange("p (h c) -> p h c", c=4)[:, :, 0:4:2]
                pairs = keys.rearrange("p (m h) c -> p m h c", h=2)
                nc.vector.tensor_copy(null_keys[:, 0:HP, part, :, :], pairs)
                nc.vector.tensor_copy(null_keys[:, HP:HP + 1, part, :, :], pairs[:, 0:1])
            dve.wait_ge(masks, 1)
            values = ps[2][:, 2 * P:2 * P + ROWS].rearrange("p (h c) -> p h c", c=4)[:, :, 1:4:2]
            for m in range(HP):
                for h in range(2):
                    ins = nc.vector.tensor_copy(nvb[DH * h:DH * h + DH, m, :, 4 * m + 2 * h:4 * m + 2 * h + 2], values[DH * h:DH * h + DH, 2 * m + h, :].unsqueeze(1).to_broadcast([DH, 4, 2]))
            ins.then_inc(nvb_ready, 1)
            dve.wait_ge(nvo_full, 1).then_inc(nvo_full, -1)
            nc.vector.tensor_tensor(nvo[:, :, :], blk[:, :, :], ps[3][:, 0:P].unsqueeze(1).to_broadcast([P, 4, P]), ALU.mult).then_inc(step, 1)
            dve.wait_ge(step, 1).then_inc(step, -1)


def attention(nc, x, ident, dram):
    gamma, w_q, w_kv, null_kv, q_scale, k_scale, w_out = dram
    HEADS, NULL, DH = null_kv.shape[0], null_kv.shape[1] // 2, null_kv.shape[2]
    NB = 4
    HP = HEADS // 2
    NT = x.shape[1] // NB
    N = NT * P
    FAR = N
    QK = 2 * P
    start = 2.0 ** (-2.0 ** (-(4 - 3.0)))
    slopes = [start * start ** i for i in range(HEADS)]
    RING = 3
    with ExitStack() as ctx:
        sb = lambda n, s, d=F32: ctx.enter_context(nc.sbuf_tensor("a_" + n, s, d))
        sem = lambda n: ctx.enter_context(nc.semaphore("a_" + n))

        xnT = sb("xnT", [P, NB, N])
        wo = sb("wo", [P, HP + 1, P])
        scales = sb("scales", [P, 1])
        dist = sb("dist", [P, FAR + P])
        null_dist = sb("null_dist", [P, NT, NULL])
        slope = sb("slope", [P, HEADS + 2])
        null_keys = sb("null_keys", [P, HP + 1, 2, 2, NULL], F32R)
        nvo = sb("nvo", [P, 4, P])

        prepare_attention(nc, x, ident, dram, (xnT, wo, scales, dist, null_dist, slope, null_keys, nvo), slopes)

        qT = [sb(f"qT{r}", [P, 2, N], F32R) for r in range(2)]
        khT = [sb(f"khT{r}", [P, 2, N], F32R) for r in range(2)]
        klT = [sb(f"klT{r}", [P, 2, N], F32R) for r in range(2)]
        qkv = [sb(f"qkv{r}", [P, NT, 3 * P]) for r in range(2)]
        null_neg = [sb(f"null_neg{r}", [P, NT, 2, NULL]) for r in range(2)]
        null_min = [sb(f"null_min{r}", [P, NT, 2]) for r in range(2)]
        w_now = sb("w_now", [P, 3 * P])
        null_now = sb("null_now", [P, 2, 2, NULL], F32R)
        slope_now = sb("slope_now", [P, 2])
        table = sb("table", [P, 2, FAR + P])
        square = sb("square", [P, NT // 2, 4, DH])
        norm2 = sb("norm2", [P, NT // 2, 4])
        rnorm = sb("rnorm", [P, NT // 2, 4])
        unit = [sb(f"unit{g}", [P, NT // 2, 4, 2, DH]) for g in range(2)]
        ntmp = sb("ntmp", [P, NT // 2, 4])
        prob = [sb(f"prob{k}", [P, 2, N]) for k in range(2)]
        probT = [sb(f"probT{k}", [P, 2, N]) for k in range(2)]
        neg_max = sb("neg_max", [P, NT, 2])
        row_sum = sb("row_sum", [P, NT, 2])
        null_arg = sb("null_arg", [P, NT // 2, 2, NULL])
        null_prob = sb("null_prob", [P, NT // 2, 2, NULL])
        total = sb("total", [P, NT // 2, 2])
        rtotal = sb("rtotal", [P, NT // 2, 2])
        rtotal_wide = sb("rtotal_wide", [P, NT // 2, 2, DH])
        null_all = sb("null_all", [P, NB, NT, 4 * HP])
        oT = sb("oT", [P, 4 * P])

        score = [ctx.enter_context(nc.psum_tensor(f"a_score{h}", [P, N], F32)) for h in range(2)]
        ring = [ctx.enter_context(nc.psum_tensor(f"a_ring{k}", [P, 4 * P], F32)) for k in range(RING)]
        outT = ctx.enter_context(nc.psum_tensor("a_outT", [P, 4 * P], F32))

        step = sem("step")
        pool_step = sem("pool_step")
        zeroed = sem("zeroed")
        score_full = [sem(f"score_full{h}") for h in range(2)]
        score_free = [sem(f"score_free{h}") for h in range(2)]
        shifted = [sem(f"shifted{h}") for h in range(2)]
        prob_ready = [sem(f"prob_ready{h}") for h in range(2)]
        to_act = [sem(f"to_act{k}") for k in range(RING)]
        to_dve = [sem(f"to_dve{k}") for k in range(RING)]
        freed = [sem(f"freed{k}") for k in range(RING)]
        high_ready = sem("high_ready")
        o_full = sem("o_full")
        o_copied = sem("o_copied")
        null_arg_ready = sem("null_arg_ready")
        null_prob_ready = sem("null_prob_ready")
        rtotal_ready = sem("rtotal_ready")
        projected = sem("projected")
        squared = sem("squared")
        summed = sem("summed")
        normed = sem("normed")
        unit_free = sem("unit_free")
        w_free = sem("w_free")
        w_loaded = sem("w_loaded")
        null_loaded = sem("null_loaded")
        nullT_ready = sem("nullT_ready")

        fill = {
            0: ([("PV", 7), ("O", 1)], [("PROJ", 0), ("PROJ", 1)], [("PROJ", 2)], [("PROJ", 3), ("RB", 1)]),
            1: ([("SQ", 0)], [], [], [("Y", 1), ("PROJ", 4), ("PROJ", 5)]),
            2: ([("RS", 0), ("PV", 0)], [], [("PV", 1), ("NM", 0), ("PROJ", 6)], []),
            3: ([], [], [("PV", 2), ("PROJ", 7)], []),
            4: ([], [("R2", 0)], [("PV", 3), ("O", 0)], [("RB", 0)]),
            5: ([("SLOPE",)], [], [("SQ", 1), ("RS", 1), ("C", 0, 0), ("C", 0, 1), ("C", 0, 2)], []),
            6: ([("Y", 0), ("PV", 4)], [], [("C", 0, 3), ("PV", 5)], [("NULL", 0), ("NM", 1), ("C", 1, 0), ("C", 1, 1), ("PV", 6)]),
            7: ([], [], [], [("NULL", 1), ("C", 1, 2), ("C", 1, 3), ("R2", 1)]),
        }
        plan = []
        for t in range(NT):
            u = (t + 1) % NT
            plan += [("S", u, 0)] + fill[t][0] + [("T", t, 0), ("S", u, 1)] + fill[t][1]
            plan += [("TAB", 0)] * (u == 0) + [("SM", u, 0), ("T", t, 1)] + [("R1", t // 4)] * (t % 4 == 3) + fill[t][2]
            plan += [("TAB", 1)] * (u == 0) + [("SM", u, 1)] + fill[t][3]
        bank, fills = {}, 0
        for s in plan:
            for g in range(1 + (s[0] == "T" and s[1] >= 4)):
                if s[0] in ("T", "C", "PROJ", "NULL", "RB", "Y"):
                    bank[s, g] = fills % RING
                    fills += 1
        first = [s for s in plan if s[0] in ("PROJ", "SQ", "RS", "NM", "C", "NULL", "SLOPE", "TAB") or s[0] in ("S", "SM") and s[1] == 0]
        rest = [("PV", 7), ("O", 1), ("RB", 1), ("Y", 1)]

        def turns(eng, run):
            run(first, -1, NB - 1)
            with eng.Fori(0, HP) as hp:
                for b in range(NB):
                    run(plan, hp, b)
            run(rest, HP, 0)

        block = ctx.enter_context(nc.Block("attention"))

        @block.sync
        def _(sp):
            def load(pair):
                for part, w in enumerate((w_q, w_kv[:, 0:HP * P], w_kv[:, HP * P:2 * HP * P])):
                    sp.dma_start(w_now[:, P * part:P * part + P].unsqueeze(1), w.rearrange("p (m n) -> p m n", n=P)[:, bass.ds(pair, 1), :]).then_inc(w_loaded, 16)

            load(0)
            with sp.Fori(1, HP) as pair:
                sp.wait_ge(w_free, 1).then_inc(w_free, -1)
                load(pair)
            sp.wait_ge(w_free, 1).then_inc(w_free, -1)
            load(0)

        @block.gpsimd
        def _(pool):
            def run(steps, hp, b):
                for s in steps:
                    if s[0] in ("SQ", "NM"):
                        four = slice(4 * s[1], 4 * s[1] + 4)
                        qk = qkv[(b + 1) % 2][:, four, 0:QK]
                    if s[0] == "SQ":
                        pool.wait_ge(projected, 1).then_inc(projected, -1)
                        nc.gpsimd.tensor_tensor(square[:, :, :, :].rearrange("p t v d -> p t (v d)"), qk, qk, ALU.mult).then_inc(squared, 1)
                    if s[0] == "NM":
                        pool.wait_ge(summed, 1).then_inc(summed, -1)
                        newton_rsqrt(nc.gpsimd, pool, pool_step, rnorm[:, :, :], norm2[:, :, :], ntmp[:, :, :])
                        vectors = qk.rearrange("p t (v d) -> p t v d", d=DH)
                        pool.wait_ge(unit_free, 1).then_inc(unit_free, -1)
                        for c in range(2):
                            ins = nc.gpsimd.tensor_tensor(unit[s[1]][:, :, :, c, :], vectors, rnorm[:, :, :].unsqueeze(3).to_broadcast([P, 4, 4, DH]), ALU.mult)
                        ins.then_inc(normed, 1)

            nc.gpsimd.memset(qkv[1][:, :, QK:3 * P], 0.0)
            nc.gpsimd.memset(rtotal_wide[:, :, :, :], 0.0).then_inc(zeroed, 1)
            turns(pool, run)

        @block.tensor
        def _(pe):
            def run(steps, hp, b):
                r, n = b % 2, (b + 1) % 2
                for s in steps:
                    if steps is first and s[0] in ("S", "NULL"):
                        for k in range(RING):
                            pe.wait_ge(freed[k], 1)
                    if s[0] == "S":
                        _, t, h = s
                        q = r if t else n
                        pe.wait_ge(score_free[h], 1).then_inc(score_free[h], -1)
                        for c in range(0, P * (t + 1), 4 * P):
                            e = min(c + 4 * P, P * (t + 1))
                            nc.tensor.matmul(score[h][:, c:e], qT[q][:, h, P * t:P * t + P], khT[q][:, h, c:e], start=True, stop=False)
                            ins = nc.tensor.matmul(score[h][:, c:e], qT[q][:, h, P * t:P * t + P], klT[q][:, h, c:e], start=False, stop=True)
                        ins.then_inc(score_full[h], 1)
                    if s[0] == "T":
                        _, t, h = s
                        pe.wait_ge(prob_ready[h], 1).then_inc(prob_ready[h], -1)
                        for g in range(1 + (t >= 4)):
                            k = bank[s, g]
                            pe.wait_ge(freed[k], 1).then_inc(freed[k], -1)
                            for j in range(4 * g, min(4 * g + 4, t + 1)):
                                ins = nc.tensor.transpose(ring[k][:, P * (j % 4):P * (j % 4) + P], prob[t % 2][:, h, P * j:P * j + P], ident[:, :])
                            ins.then_inc((to_act, to_dve)[h][k], 1)
                    if s[0] == "PV":
                        t = s[1]
                        v = qkv[n if t == 7 else r]
                        if steps is rest:
                            for k in range(RING):
                                pe.wait_ge(freed[k], 1)
                        for j in range(t + 1):
                            for h in range(2):
                                ins = nc.tensor.matmul(outT[DH * h:DH * h + DH, P * (t % 4):P * (t % 4) + P], v[:, j, QK + DH * h:QK + DH * h + DH], probT[t % 2][:, h, P * j:P * j + P], start=(j == 0), stop=(j == t))
                        if t % 4 == 3:
                            ins.then_inc(o_full, 1)
                    if s[0] == "RB":
                        k = bank[s, 0]
                        pe.wait_ge(rtotal_ready, 1).then_inc(rtotal_ready, -1)
                        pe.wait_ge(freed[k], 1).then_inc(freed[k], -1)
                        for t in range(4):
                            ins = nc.tensor.transpose(ring[k][:, P * t:P * t + P], rtotal_wide[:, t, :, :], ident[:, :])
                        ins.then_inc(to_dve[k], 1)
                    if s[0] == "Y":
                        k = bank[s, 0]
                        if steps is rest:
                            pe.wait_ge(freed[bank[("RB", 1), 0]], 1)
                        pe.wait_ge(freed[k], 1).then_inc(freed[k], -1)
                        pair = hp + 1 if s[1] == 0 or b > 0 else hp
                        for t in range(4):
                            ins = nc.tensor.matmul(ring[k][:, P * t:P * t + P], oT[:, P * t:P * t + P], wo[:, bass.ds(pair, 1), :], start=True, stop=True)
                        ins.then_inc(to_dve[k], 1)
                    if s[0] == "PROJ":
                        t = s[1]
                        k = bank[s, 0]
                        if t == 0 and b == NB - 1:
                            pe.wait_ge(w_loaded, 3 * 16).then_inc(w_loaded, -3 * 16)
                        pe.wait_ge(freed[k], 1).then_inc(freed[k], -1)
                        nc.tensor.matmul(ring[k][:, 0:3 * P], xnT[:, (b + 1) % NB, P * t:P * t + P], w_now[:, :], start=True, stop=True).then_inc(to_act[k], 1)
                    if s[0] == "C":
                        _, g, vec = s
                        k = bank[s, 0]
                        if vec == 0:
                            pe.wait_ge(normed, 1).then_inc(normed, -1)
                        pe.wait_ge(freed[k], 1).then_inc(freed[k], -1)
                        for t in range(4):
                            ins = nc.tensor.transpose(ring[k][:, P * t:P * t + P], unit[g][:, t, vec, :, :], ident[:, :])
                        ins.then_inc(to_act[k], 1)
                    if s[0] == "NULL":
                        g = s[1]
                        k = bank[s, 0]
                        if g == 0 and b == NB - 1:
                            pe.wait_ge(null_loaded, 1).then_inc(null_loaded, -1)
                        pe.wait_ge(freed[k], 1).then_inc(freed[k], -1)
                        for t in range(4):
                            for h in range(2):
                                c = 2 * NULL * (2 * t + h)
                                ins = nc.tensor.matmul(ring[k][:, c:c + 2 * NULL], qT[n][:, h, P * (4 * g + t):P * (4 * g + t) + P], null_now[:, :, h, :], start=True, stop=True)
                        ins.then_inc(to_dve[k], 1)

            for k in range(RING):
                pe.sem_inc(freed[k], 1)
            for h in range(2):
                pe.sem_inc(score_free[h], 1)
            pe.wait_ge(zeroed, 2)
            pe.sem_inc(rtotal_ready, 1)
            turns(pe, run)
            for k in range(RING):
                pe.wait_ge(freed[k], 1)
            for half in range(2):
                for n in range(4):
                    b, g = 2 * half + n // 2, n % 2
                    ins = nc.tensor.transpose(ring[0][:, P * n:P * n + P], null_all[:, b, 4 * g:4 * g + 4, :], ident[:, :])
                ins.then_inc(to_act[0], 1)
                pe.wait_ge(nullT_ready, 1).then_inc(nullT_ready, -1)
                for n in range(4):
                    k = 1 + n % 2
                    pe.wait_ge(freed[k], 1).then_inc(freed[k], -1)
                    nc.tensor.matmul(ring[k][:, :], oT[:, P * n:P * n + P], nvo[:, :, :], start=True, stop=True).then_inc(to_dve[k], 1)

        @block.scalar
        def _(act):
            def run(steps, hp, b):
                n = (b + 1) % 2
                for s in steps:
                    if s[0] == "T" and s[2] == 0:
                        t = s[1]
                        for g in range(1 + (t >= 4)):
                            k = bank[s, g]
                            c, e = 4 * P * g, min(4 * P * (g + 1), P * (t + 1))
                            act.wait_ge(to_act[k], 1).then_inc(to_act[k], -1)
                            nc.scalar.copy(probT[t % 2][:, 0, c:e], ring[k][:, 0:e - c]).then_inc(freed[k], 1)
                    if s[0] == "SM":
                        _, t, h = s
                        p = prob[t % 2][:, h, 0:P * (t + 1)]
                        act.wait_ge(shifted[h], 1).then_inc(shifted[h], -1)
                        act.sem_inc(score_free[h], 1)
                        nc.scalar.activation(p, p, ACT.Exp, bias=neg_max[:, t, h:h + 1], scale=-1.0, accum_out=row_sum[:, t, h:h + 1]).then_inc(prob_ready[h], 1)
                    if s[0] == "R1":
                        act.wait_ge(null_arg_ready, 1).then_inc(null_arg_ready, -1)
                        nc.scalar.activation(null_prob[:, :, :, :], null_arg[:, :, :, :], ACT.Exp).then_inc(null_prob_ready, 1)
                    if s[0] == "O":
                        act.wait_ge(o_full, 1).then_inc(o_full, -1)
                        nc.scalar.copy(oT[:, :], outT[:, :]).then_inc(o_copied, 1)
                    if s[0] == "PROJ":
                        k = bank[s, 0]
                        act.wait_ge(to_act[k], 1).then_inc(to_act[k], -1)
                        if s[1] % 4 == 3:
                            nc.scalar.copy(qkv[n][:, s[1], 0:QK], ring[k][:, 0:QK]).then_inc(projected, 1)
                            nc.scalar.copy(qkv[n][:, s[1], QK:3 * P], ring[k][:, QK:3 * P]).then_inc(freed[k], 1)
                        else:
                            nc.scalar.copy(qkv[n][:, s[1], :], ring[k][:, 0:3 * P]).then_inc(freed[k], 1)
                        if s[1] == NT - 1 and b == NB - 2:
                            act.sem_inc(w_free, 1)
                    if s[0] == "C":
                        _, g, vec = s
                        k = bank[s, 0]
                        act.wait_ge(to_act[k], 1).then_inc(to_act[k], -1)
                        if vec == 3:
                            act.sem_inc(unit_free, 1)
                        high = (qT, khT)[vec // 2][n][:, vec % 2, 4 * P * g:4 * P * g + 4 * P]
                        nc.scalar.activation(high, ring[k][:, :], ACT.Copy, scale=1.0 if vec < 2 else scales[:, 0:1]).then_inc(high_ready, 1)

            act.sem_inc(unit_free, 2)
            turns(act, run)
            for half in range(2):
                act.wait_ge(to_act[0], 1).then_inc(to_act[0], -1)
                nc.scalar.copy(oT[:, :], ring[0][:, :]).then_inc(nullT_ready, 1)

        @block.vector
        def _(dve):
            def run(steps, hp, b):
                r, n = b % 2, (b + 1) % 2
                for s in steps:
                    if s[0] == "T" and s[2] == 1:
                        t = s[1]
                        for g in range(1 + (t >= 4)):
                            k = bank[s, g]
                            c, e = 4 * P * g, min(4 * P * (g + 1), P * (t + 1))
                            dve.wait_ge(to_dve[k], 1).then_inc(to_dve[k], -1)
                            nc.vector.tensor_copy(probT[t % 2][:, 1, c:e], ring[k][:, 0:e - c]).then_inc(freed[k], 1)
                    if s[0] == "SM":
                        _, t, h = s
                        w, q = P * (t + 1), r if t else n
                        dve.wait_ge(score_full[h], 1).then_inc(score_full[h], -1)
                        nc.vector.tensor_tensor_reduce(out=prob[t % 2][:, h, 0:w], in0=score[h][:, 0:w], in1=table[:, h, FAR - P * t:FAR + P], scale=-1.0, scalar=null_min[q][:, t, h:h + 1], op0=ALU.add, op1=ALU.min, accum_out=neg_max[:, t, h:h + 1]).then_inc(shifted[h], 1)
                    if s[0] == "R1":
                        g = 4 * s[1]
                        nc.vector.tensor_tensor(null_arg[:, :, :, :], neg_max[:, g:g + 4, :].unsqueeze(3).to_broadcast([P, 4, 2, NULL]), null_neg[r][:, g:g + 4, :, :], ALU.subtract).then_inc(null_arg_ready, 1)
                    if s[0] == "R2":
                        g = 4 * s[1]
                        dve.wait_ge(null_prob_ready, 1).then_inc(null_prob_ready, -1)
                        nc.vector.tensor_reduce(total[:, :, :], null_prob[:, :, :, :], AX.X, ALU.add).then_inc(step, 1)
                        dve.wait_ge(step, 1).then_inc(step, -1)
                        nc.vector.tensor_tensor(total[:, :, :], total[:, :, :], row_sum[:, g:g + 4, :], ALU.add).then_inc(step, 1)
                        dve.wait_ge(step, 1).then_inc(step, -1)
                        nc.vector.reciprocal(rtotal[:, :, :], total[:, :, :]).then_inc(step, 1)
                        dve.wait_ge(step, 1).then_inc(step, -1)
                        nc.vector.tensor_copy(rtotal_wide[:, :, :, :], rtotal[:, :, :].unsqueeze(3).to_broadcast([P, 4, 2, DH]))
                        nc.vector.tensor_tensor(null_all[:, b:b + 1, g:g + 4, bass.ds(4 * hp, 4)].rearrange("p a t (h c) -> p (a t) h c", h=2), null_prob[:, :, :, :], rtotal[:, :, :].unsqueeze(3).to_broadcast([P, 4, 2, NULL]), ALU.mult).then_inc(rtotal_ready, 1)
                    if s[0] == "RB":
                        k = bank[s, 0]
                        dve.wait_ge(to_dve[k], 1).then_inc(to_dve[k], -1)
                        dve.wait_ge(o_copied, 1).then_inc(o_copied, -1)
                        nc.vector.tensor_tensor(oT[:, :], oT[:, :], ring[k][:, :], ALU.mult).then_inc(freed[k], 1)
                    if s[0] == "Y":
                        k = bank[s, 0]
                        batch = b if s[1] == 0 else (b - 1) % NB
                        dve.wait_ge(to_dve[k], 1).then_inc(to_dve[k], -1)
                        tiles = x[:, batch * NT + 4 * s[1]:batch * NT + 4 * s[1] + 4, :]
                        nc.vector.tensor_tensor(tiles, tiles, ring[k][:, :].rearrange("p (t d) -> p t d", t=4), ALU.add).then_inc(freed[k], 1)
                    if s[0] == "RS":
                        dve.wait_ge(squared, 1).then_inc(squared, -1)
                        nc.vector.tensor_reduce(norm2[:, :, :], square[:, :, :, :], AX.X, ALU.add).then_inc(step, 1)
                        dve.wait_ge(step, 1).then_inc(step, -1)
                        nc.vector.tensor_scalar(norm2[:, :, :], norm2[:, :, :], 1e-24, None, ALU.max).then_inc(summed, 1)
                    if s[0] == "C":
                        _, g, vec = s
                        k = bank[s, 0]
                        c = slice(4 * P * g, 4 * P * g + 4 * P)
                        dve.wait_ge(high_ready, 1).then_inc(high_ready, -1)
                        if vec < 2:
                            nc.vector.tensor_tensor(qT[n][DH:P, vec, c], ring[k][DH:P, :], qT[n][DH:P, vec, c].bitcast(F32), ALU.subtract).then_inc(freed[k], 1)
                        else:
                            nc.vector.scalar_tensor_tensor(klT[n][:, vec - 2, c], ring[k][:, :], scales[:, 0:1], khT[n][:, vec - 2, c].bitcast(F32), ALU.mult, ALU.subtract).then_inc(freed[k], 1)
                    if s[0] == "SLOPE" and b == NB - 1:
                        nc.vector.tensor_copy(null_now[:, :, :, :].unsqueeze(1), null_keys[:, bass.ds(hp + 1, 1), :, :, :].bitcast(F32)).then_inc(null_loaded, 1)
                        nc.vector.tensor_copy(slope_now[:, :], slope[:, bass.ds(2 * (hp + 1), 2)]).then_inc(step, 1)
                        dve.wait_ge(step, 1).then_inc(step, -1)
                    if s[0] == "TAB" and b == NB - 1:
                        nc.vector.tensor_scalar(table[:, s[1], :], dist[:, :], slope_now[:, s[1]:s[1] + 1], None, ALU.mult).then_inc(step, 1)
                        dve.wait_ge(step, 1).then_inc(step, -1)
                    if s[0] == "NULL":
                        k = bank[s, 0]
                        g = slice(4 * s[1], 4 * s[1] + 4)
                        dve.wait_ge(to_dve[k], 1).then_inc(to_dve[k], -1)
                        o = ring[k][:, 0:4 * 4 * NULL].rearrange("p (t h s c) -> p t h s c", h=2, s=2, c=NULL)
                        for h in range(2):
                            ins = nc.vector.scalar_tensor_tensor(null_neg[n][:, g, h, :], null_dist[:, g, :], slope_now[:, h:h + 1], o[:, :, h, 0, :], ALU.mult, ALU.subtract)
                        ins.then_inc(step, 1)
                        dve.wait_ge(step, 1).then_inc(step, -1)
                        nc.vector.tensor_tensor(null_neg[n][:, g, :, :], null_neg[n][:, g, :, :], o[:, :, :, 1, :], ALU.subtract).then_inc(step, 1)
                        dve.wait_ge(step, 1).then_inc(step, -1)
                        nc.vector.tensor_reduce(null_min[n][:, g, :], null_neg[n][:, g, :, :], AX.X, ALU.min).then_inc(step, 1)
                        dve.wait_ge(step, 1).then_inc(step, -1)
                        dve.sem_inc(freed[k], 1)

            nc.vector.memset(probT[1][:, :, :], 0.0)
            nc.vector.memset(outT[:, :], 0.0).then_inc(zeroed, 1)
            turns(dve, run)
            for b in range(NB):
                for g in range(2):
                    k = 1 + g
                    dve.wait_ge(to_dve[k], 1).then_inc(to_dve[k], -1)
                    tiles = x[:, b * NT + 4 * g:b * NT + 4 * g + 4, :]
                    nc.vector.tensor_tensor(tiles, tiles, ring[k][:, :].rearrange("p (t d) -> p t d", t=4), ALU.add).then_inc(freed[k], 1)


def build(nc, args, out):
    (x_d, gamma, w_q, w_kv, null_kv, q_scale, k_scale, w_out, Wc, bc, W1, b1, W2, b2) = args
    with ExitStack() as ctx:
        sb = lambda n, s, d=F32: ctx.enter_context(nc.sbuf_tensor(n, s, d))
        sem = lambda n: ctx.enter_context(nc.semaphore(n))
        x = sb("x", [P, 32, P])
        ident = sb("ident", [P, P])
        x_loaded = sem("x_loaded")
        ident_zero = sem("ident_zero")
        ident_made = sem("ident_made")
        stored = sem("stored")
        xv = x_d.rearrange("b (t p) d -> p (b t) d", p=P)
        ov = out.rearrange("b (t p) d -> p (b t) d", p=P)
        with nc.Block("start") as block:
            @block.sync
            def _(sp):
                sp.dma_start(x[:, :, :], xv).then_inc(x_loaded, 16)
                sp.wait_ge(x_loaded, 16)

            @block.gpsimd
            def _(pool):
                nc.gpsimd.memset(ident[:, :], 0.0).then_inc(ident_zero, 1)
                pool.wait_ge(ident_zero, 1)
                nc.gpsimd.affine_select(out=ident[:, :], in_=ident[:, :], compare_op=ALU.not_equal, fill=1.0, base=0, pattern=[[-1, P]], channel_multiplier=1).then_inc(ident_made, 1)
                pool.wait_ge(ident_made, 1)
        ffn(nc, x, ident, (Wc, bc, W1, b1, W2, b2), "f1_")
        attention(nc, x, ident, (gamma, w_q, w_kv, null_kv, q_scale, k_scale, w_out))
        ffn(nc, x, ident, (Wc, bc, W1, b1, W2, b2), "f2_")
        with nc.Block("end") as block:
            @block.sync
            def _(sp):
                sp.dma_start(ov, x[:, :, :]).then_inc(stored, 16)
                sp.wait_ge(stored, 16)


_INS = ['L0_attn_x', 'L0_attn_gamma', 'L0_attn_w_q', 'L0_attn_w_kv', 'L0_attn_null_kv', 'L0_attn_q_scale',
        'L0_attn_k_scale', 'L0_attn_w_out', 'L0_ffn_Wc', 'L0_ffn_bc', 'L0_ffn_W1', 'L0_ffn_b1', 'L0_ffn_W2', 'L0_ffn_b2']


def kernel(**inputs):
    import numpy as np
    import concourse.bacc as bacc
    from concourse.bass_utils import run_bass_kernel_spmd

    nc = bacc.Bacc("TRN2", target_bir_lowering=False, num_devices=1)
    arrays, args = {}, []
    for name in _INS:
        a = np.ascontiguousarray(inputs[name])
        arrays[f"in_{name}"] = a
        args.append(nc.dram_tensor(f"in_{name}", a.shape, mybir.dt.from_np(a.dtype), kind="ExternalInput").ap())
    out = nc.dram_tensor("out_x", inputs['L0_attn_x'].shape, F32, kind="ExternalOutput").ap()
    build(nc, args, out)
    r = run_bass_kernel_spmd(nc, [arrays], core_ids=[0])
    return r.results[0]["out_x"]
```
